# Optimizing a Trainium2 kernel written in Bass

```python
import numpy as np
import jax
import jax.numpy as jnp

def _softmax(x, axis=-1):
    return jax.nn.softmax(x, axis=axis)

def _gelu(x):
    return jax.nn.gelu(x, approximate=True)

def _silu(x):
    return jax.nn.silu(x)

def _sigmoid(x):
    return jax.nn.sigmoid(x)

def _layernorm(x, axis=-1, eps=1e-05):
    m = jnp.mean(x, axis=axis, keepdims=True)
    v = jnp.var(x, axis=axis, keepdims=True)
    return (x - m) / jnp.sqrt(v + eps)

def _scatter_add(tgt, idx, src, axis=0):
    return tgt.at[idx].add(src)

def _segment_sum(src, seg, n):
    return jax.ops.segment_sum(src, seg, n)
kernel_name = 'mk_macaron_d1_jaxref_r8_63a2c7'

def setup_inputs(seed: int=0):
    np.random.seed(seed)
    _w = jnp.asarray

    def _L0_attn_setup():
        import jax, jax.numpy as jnp
        import numpy as np
        HEADS = 16
        DIM_HEAD = 64
        key = jax.random.key(seed)
        ks = jax.random.split(key, 5)
        b, n, dim = (4, 256, 128)
        return {'x': jax.random.normal(ks[0], (b, n, dim), dtype=jnp.float32), 'Wq': jax.random.normal(ks[1], (dim, HEADS * DIM_HEAD), dtype=jnp.float32) * dim ** (-0.5), 'Wkv': jax.random.normal(ks[2], (dim, DIM_HEAD), dtype=jnp.float32) * dim ** (-0.5), 'null_kv': jax.random.normal(ks[3], (DIM_HEAD,), dtype=jnp.float32), 'Wout': jax.random.normal(ks[4], (HEADS * DIM_HEAD, dim), dtype=jnp.float32) * (HEADS * DIM_HEAD) ** (-0.5)}
    _L0_attn_in = _L0_attn_setup()

    def _L0_ffn_setup():
        import jax, jax.numpy as jnp
        import numpy as np
        N_HEADS = 16
        NUM_EXPERTS = 4
        TOP_K = 2
        D_MODEL = 128
        GATE_HID = 128
        key = jax.random.key(seed)
        ks = jax.random.split(key, 12)
        B, T, C, E = (2, 128, D_MODEL, NUM_EXPERTS)
        s = 1.0 / np.sqrt(C)
        return {'hidden_states': jax.random.normal(ks[0], (B, T, C), jnp.float32), 'Wq': jax.random.normal(ks[1], (E, C, C), jnp.float32) * s, 'bq': jnp.zeros((E, C), jnp.float32), 'Wk': jax.random.normal(ks[2], (E, C, C), jnp.float32) * s, 'bk': jnp.zeros((E, C), jnp.float32), 'Wv': jax.random.normal(ks[3], (E, C, C), jnp.float32) * s, 'bv': jnp.zeros((E, C), jnp.float32), 'Wg1': jax.random.normal(ks[4], (C, GATE_HID), jnp.float32) * s, 'bg1': jnp.zeros((GATE_HID,), jnp.float32), 'Wg2': jax.random.normal(ks[5], (GATE_HID, E), jnp.float32) / np.sqrt(GATE_HID), 'bg2': jnp.zeros((E,), jnp.float32), 'Wo': jax.random.normal(ks[6], (C, C), jnp.float32) * s, 'bo': jnp.zeros((C,), jnp.float32)}
    _L0_ffn_in = _L0_ffn_setup()
    _d = {'L0_attn_x': _L0_attn_in['x'], 'L0_attn_Wq': _L0_attn_in['Wq'], 'L0_attn_Wkv': _L0_attn_in['Wkv'], 'L0_attn_null_kv': _L0_attn_in['null_kv'], 'L0_attn_Wout': _L0_attn_in['Wout'], 'L0_ffn_Wq': _L0_ffn_in['Wq'], 'L0_ffn_bq': _L0_ffn_in['bq'], 'L0_ffn_Wk': _L0_ffn_in['Wk'], 'L0_ffn_bk': _L0_ffn_in['bk'], 'L0_ffn_Wv': _L0_ffn_in['Wv'], 'L0_ffn_bv': _L0_ffn_in['bv'], 'L0_ffn_Wg1': _L0_ffn_in['Wg1'], 'L0_ffn_bg1': _L0_ffn_in['bg1'], 'L0_ffn_Wg2': _L0_ffn_in['Wg2'], 'L0_ffn_bg2': _L0_ffn_in['bg2'], 'L0_ffn_Wo': _L0_ffn_in['Wo'], 'L0_ffn_bo': _L0_ffn_in['bo']}
    _x0 = _d['L0_attn_x']
    _d['L0_attn_x'] = jax.random.normal(jax.random.fold_in(jax.random.key(seed), 1), (2, 1024, 128), dtype=_x0.dtype)
    del _x0
    return _d

def reference(L0_attn_x, L0_attn_Wq, L0_attn_Wkv, L0_attn_null_kv, L0_attn_Wout, L0_ffn_Wq, L0_ffn_bq, L0_ffn_Wk, L0_ffn_bk, L0_ffn_Wv, L0_ffn_bv, L0_ffn_Wg1, L0_ffn_bg1, L0_ffn_Wg2, L0_ffn_bg2, L0_ffn_Wo, L0_ffn_bo):

    def _L0_attn_ref(x, Wq, Wkv, null_kv, Wout):
        import jax, jax.numpy as jnp
        import numpy as np
        HEADS = 16
        DIM_HEAD = 64
        b, n, dim = x.shape
        scale = DIM_HEAD ** (-0.5)
        q = (x @ Wq).reshape(b, n, HEADS, DIM_HEAD).transpose(0, 2, 1, 3) * scale
        kv = x @ Wkv
        kv = jnp.concatenate([jnp.broadcast_to(null_kv, (b, 1, DIM_HEAD)), kv], axis=1)
        sim = jnp.einsum('bhid,bjd->bhij', q, kv)
        mask_value = -jnp.finfo(sim.dtype).max
        i, j = (sim.shape[-2], sim.shape[-1])
        causal_mask = jnp.triu(jnp.ones((i, j), dtype=bool), k=j - i + 1)
        sim = jnp.where(causal_mask, mask_value, sim)
        attn = jax.nn.softmax(sim.astype(jnp.float32), axis=-1)
        out = jnp.einsum('bhij,bjd->bhid', attn, kv.astype(jnp.float32))
        out = out.transpose(0, 2, 1, 3).reshape(b, n, HEADS * DIM_HEAD)
        return out @ Wout

    def _L0_ffn_ref(hidden_states, Wq, bq, Wk, bk, Wv, bv, Wg1, bg1, Wg2, bg2, Wo, bo):
        import jax, jax.numpy as jnp
        import numpy as np
        N_HEADS = 16
        NUM_EXPERTS = 4
        TOP_K = 2
        D_MODEL = 128
        GATE_HID = 128
        B, T, C = hidden_states.shape
        H = N_HEADS
        D = C // H
        pooled = hidden_states.mean(axis=1)
        logits = jax.nn.relu(pooled @ Wg1 + bg1) @ Wg2 + bg2
        vals, idx = jax.lax.top_k(logits, TOP_K)
        sm = jax.nn.softmax(vals, axis=-1)
        weights = jnp.zeros_like(logits).at[jnp.arange(B)[:, None], idx].set(sm)

        def moe_proj(W, b):
            Wc = jnp.einsum('be,ecd->bcd', weights, W)
            bc = weights @ b
            return jnp.einsum('btc,bcd->btd', hidden_states, Wc) + bc[:, None, :]
        q = moe_proj(Wq, bq).reshape(B, T, H, D)
        k = moe_proj(Wk, bk).reshape(B, T, H, D)
        v = moe_proj(Wv, bv).reshape(B, T, H, D)
        scores = jnp.einsum('bthd,bshd->bhts', q, k) / np.sqrt(D).astype(np.float32)
        attn = jax.nn.softmax(scores, axis=-1)
        out = jnp.einsum('bhts,bshd->bthd', attn, v).reshape(B, T, C)
        return out @ Wo + bo
    x = L0_attn_x
    x = x + 0.5 * _L0_ffn_ref(_layernorm(x, axis=-1), L0_ffn_Wq, L0_ffn_bq, L0_ffn_Wk, L0_ffn_bk, L0_ffn_Wv, L0_ffn_bv, L0_ffn_Wg1, L0_ffn_bg1, L0_ffn_Wg2, L0_ffn_bg2, L0_ffn_Wo, L0_ffn_bo)
    x = x + _L0_attn_ref(_layernorm(x, axis=-1), L0_attn_Wq, L0_attn_Wkv, L0_attn_null_kv, L0_attn_Wout)
    x = x + 0.5 * _L0_ffn_ref(_layernorm(x, axis=-1), L0_ffn_Wq, L0_ffn_bq, L0_ffn_Wk, L0_ffn_bk, L0_ffn_Wv, L0_ffn_bv, L0_ffn_Wg1, L0_ffn_bg1, L0_ffn_Wg2, L0_ffn_bg2, L0_ffn_Wo, L0_ffn_bo)
    return x

_drawn_inputs = setup_inputs


def setup_inputs(seed=0):
    import zlib

    import numpy as np

    out = dict(_drawn_inputs(seed))
    spreads = {'L0_ffn_bq': (0.0, 0.8),
     'L0_ffn_bk': (0.0, 2.0),
     'L0_ffn_bv': (0.0, 0.1),
     'L0_ffn_bg1': (0.0, 2.0),
     'L0_ffn_bg2': (0.0, 0.8),
     'L0_ffn_bo': (0.0, 0.1)}
    factors = {'L0_ffn_Wg1': 8.0}
    for name, (base, spread) in spreads.items():
        noise = np.random.default_rng([zlib.crc32(name.encode()), seed]).standard_normal(out[name].shape)
        drawn = base * np.exp(spread * noise) if base else spread * noise
        out[name] = jnp.asarray(drawn.astype(out[name].dtype))
    for name, factor in factors.items():
        out[name] = (out[name] * factor).astype(out[name].dtype)
    return out
```

```python
from contextlib import ExitStack

import concourse.bass as bass
from concourse import mybir

F32 = mybir.dt.float32
BF16 = mybir.dt.bfloat16
ALU = mybir.AluOpType
ACT = mybir.ActivationFunctionType
AX = mybir.AxisListType.X

P = 128
C = 128
EPS = 1e-5


def build(nc, x_in, a_wq, a_wkv, a_null, a_wout, f_wq, f_bq, f_wk, f_bk, f_wv, f_bv,
          f_wg1, f_bg1, f_wg2, f_bg2, f_wo, f_bo, out):
    B, T, _ = x_in.shape
    NT = T // P
    HALF = 512
    E = f_wq.shape[0]
    FH = 16
    FD = C // FH
    F_SCALE = float(FD) ** -0.5
    UNITS = B * FH
    NB = 4
    SHIFT = 7
    AH, AD = 16, a_wkv.shape[1]
    PAIRS = AH // 2
    A_SCALE = float(AD) ** -0.5
    KEYS = T + 1
    RING = 8
    A_LAG = 4
    MASKED = -1e30

    with ExitStack() as ctx:
        def sb(name, shape, dt=F32):
            return ctx.enter_context(nc.sbuf_tensor(name, shape, dt))

        def sem(name):
            return ctx.enter_context(nc.semaphore(name))

        q_parts_dram = nc.dram_tensor("q_parts_dram", [UNITS, 3, FD, T], BF16)
        k_parts_dram = nc.dram_tensor("k_parts_dram", [UNITS, 3, FD, T], BF16)
        o_dram = nc.dram_tensor("o_dram", [UNITS, 4, 2 * FD, HALF], F32)

        x = sb("x", [P, B * NT, C])
        xn = sb("xn", [P, NT, C])
        xnT = sb("xnT", [P, B, T])
        stats = sb("stats", [P, B * NT, 6])
        mean_var = sb("mean_var", [P, B * NT, 2])
        rstd = sb("rstd", [P, B * NT])
        ident = sb("ident", [P, P])
        eps_col = sb("eps_col", [P, 1])
        ytmp = sb("ytmp", [P, 4, C])

        w_experts = sb("w_experts", [P, E, 4, C])
        w_mix = sb("w_mix", [P, B, 4, C])
        b_experts = sb("b_experts", [P, 2, E])
        b_mix = sb("b_mix", [P, B, 2])
        wg1 = sb("wg1", [P, C])
        wg2 = sb("wg2", [P, E])
        bg1 = sb("bg1", [P, 1])
        bg2 = sb("bg2", [P, E])
        wo = sb("wo", [P, C])
        bo = sb("bo", [P, C])
        tok_sum = sb("tok_sum", [P, B, 2])
        hid = sb("hid", [P, P])
        tri = sb("tri", [P, E, E])
        lg = sb("lg", [P, E])
        g_cmp = sb("g_cmp", [P, E, E])
        g_eq = sb("g_eq", [P, E, E])
        g_s = sb("g_s", [P, 8, E])
        gate = sb("gate", [P, B, E])

        v_unit = sb("v_unit", [P, NB, NT, 32])
        neg_max = sb("neg_max", [P, NB, NT])
        max_parts = sb("max_parts", [P, 32], BF16)
        max_T = sb("max_T", [P, 32], BF16)

        wkv2 = sb("wkv2", [P, 2, AD])
        wout = sb("wout", [P, PAIRS, C])
        null_col = sb("null_col", [P, 1])
        null_sel = sb("null_sel", [P, PAIRS * AH])
        null_out = sb("null_out", [AH, C])
        ident_bf = sb("ident_bf", [P, P], BF16)
        causal = sb("causal", [P, P], BF16)
        wq_pair = sb("wq_pair", [P, 2, 2 * AD])
        a_neg_max = sb("a_neg_max", [P, 2 * NT])
        a_sum = sb("a_sum", [P, 2 * NT])
        a_rsum = sb("a_rsum", [P, 2 * NT])
        p0 = sb("p0", [P, NT, AH])
        p0_T = sb("p0_T", [AH, T])

        ARENA = 154 * 256
        arena = sb("arena", [P, ARENA])
        at = [0]

        def carve(shape, dt=F32, pattern=None, **dims):
            n = 1
            for k in shape:
                n *= k
            words = n if dt == F32 else (n + 1) // 2
            flat = arena[:, at[0]:at[0] + words]
            at[0] += words
            assert at[0] <= ARENA, at[0]
            if dt != F32:
                flat = flat.bitcast(dt)[:, 0:n]
            if len(shape) == 1:
                return flat
            names = "abcdef"[:len(shape)]
            return flat.rearrange(f"p ({' '.join(names)}) -> p {' '.join(names)}", **dict(zip(names, shape)))

        qkf = carve([2, T])
        qkr = carve([2, T])
        parts = carve([2, 3, T], BF16)
        v_all = carve([UNITS, NT, FD])
        probs = carve([2 * NT, HALF])
        o_unit = carve([2, HALF])
        o_all = carve([2, 2, T])
        num = carve([T])
        den = carve([T])
        q_stack = carve([NB, T], BF16)
        k_stack = carve([NB, T], BF16)
        at[0] = 0
        k_a = carve([KEYS + 1], BF16)
        k_b = carve([KEYS + 1], BF16)
        av = carve([NT, AD])
        q_part = carve([3, T], BF16)
        q_rest = carve([T])
        q_s = carve([2, 2, 3, T], BF16)
        a_probs = carve([RING, KEYS + 3])
        probs_T = [carve([2, 4 * (qh + 1), HALF]) for qh in range(2)]
        o_T = carve([PAIRS, T])
        at[0] -= PAIRS * T
        kvf = carve([KEYS + 1])
        kvr = carve([KEYS + 1])

        ps = ctx.enter_context(nc.psum_tensor("ps", [P, 8, HALF], F32))
        EXP_BANK = [0, 1, 2] * 5 + [1]
        MAX_BANK = [3, 5]
        PV_BANK = 7
        S_BANK = [3, 0]
        T_BANK = [5, 6]

        w_loaded = sem("w_loaded")
        aw_loaded = sem("aw_loaded")
        wq_loaded = [sem(f"wq_loaded_{k}") for k in range(2)]
        act_waited = sem("act_waited")
        kv_done = sem("kv_done")
        av_done = sem("av_done")
        av_ready = sem("av_ready")
        kvf_ready = sem("kvf_ready")
        kvr_ready = sem("kvr_ready")
        k_split = sem("k_split")
        k3_ready = sem("k3_ready")
        keys_ready = sem("keys_ready")
        proj_done = sem("proj_done")
        q1_ready = sem("q1_ready")
        q2_ready = sem("q2_ready")
        q3_ready = sem("q3_ready")
        pv_bank_free = sem("pv_bank_free")
        q_s_loaded = [sem(f"q_s_loaded_{k}") for k in range(2)]
        a_scores = sem("a_scores")
        a_max = sem("a_max")
        a_exp = sem("a_exp")
        a_rsum_ready = sem("a_rsum_ready")
        p0_ready = sem("p0_ready")
        a_normed = sem("a_normed")
        tr_done = [sem(f"tr_done_{k}") for k in range(2)]
        evac_dve = sem("evac_dve")
        evac_act = sem("evac_act")
        apv_done = sem("apv_done")
        p0T_done = sem("p0T_done")
        p0T_ready = sem("p0T_ready")
        null_done = sem("null_done")
        null_ready = sem("null_ready")
        ay_done = sem("ay_done")
        x_loaded = [sem(f"x_loaded_{b}") for b in range(B)]
        const_ready = sem("const_ready")
        eps_ready = sem("eps_ready")
        dve_link = sem("dve_link")
        mv_ready = sem("mv_ready")
        std_ready = sem("std_ready")
        xn_ready = sem("xn_ready")
        xT_done = sem("xT_done")
        xnT_ready = sem("xnT_ready")
        hid_done = sem("hid_done")
        hid_ready = sem("hid_ready")
        logits_done = sem("logits_done")
        gexp_in = sem("gexp_in")
        gexp_out = sem("gexp_out")
        mix_ready = sem("mix_ready")
        qk_done = sem("qk_done")
        vproj_done = sem("vproj_done")
        qkf_ready = sem("qkf_ready")
        v_ready = sem("v_ready")
        part1_ready = sem("part1_ready")
        rest_ready = sem("rest_ready")
        part2_ready = sem("part2_ready")
        part3_ready = sem("part3_ready")
        parts_stored = sem("parts_stored")
        pool_waited = sem("pool_waited")
        stacks_loaded = [sem(f"stacks_loaded_{g}") for g in range(NB)]
        rows_zeroed = sem("rows_zeroed")
        stacks_clear = sem("stacks_clear")
        v_unit_ready = sem("v_unit_ready")
        max_scores = sem("max_scores")
        max_read = sem("max_read")
        max_T_ready = sem("max_T_ready")
        max_link = sem("max_link")
        max_rows = sem("max_rows")
        scores_done = sem("scores_done")
        probs_ready = sem("probs_ready")
        pv_done = sem("pv_done")
        o_ready = sem("o_ready")
        o_stored = [sem(f"o_stored_{g}") for g in range(2)]
        o_loaded = sem("o_loaded")
        on_ready = sem("on_ready")
        y_done = sem("y_done")
        x_ready = sem("x_ready")
        out_stored = sem("out_stored")

        N_W = 14
        STEPS = [(qh, hh, 4 * qh + k) for qh in range(2) for hh in range(2) for k in range(4)]
        NS = len(STEPS)
        USES = [[(k, min(4, qt + 1 - k)) for k in range(0, qt + 1, 4)] for _, _, qt in STEPS]
        FIRST_USE = [sum(len(USES[s]) for s in range(t)) for t in range(NS)]
        Q_STEPS = (A_LAG + 2, A_LAG + 4)
        N_USES = sum(len(v) for v in USES)

        TB = 2 * NT

        block = ctx.enter_context(nc.Block())

        @block.sync
        def _(sp):
            for b in range(B):
                sp.dma_start(x[:, b * NT:(b + 1) * NT, :], x_in[b].rearrange("(t p) c -> p t c", p=P)).then_inc(x_loaded[b], 16)
            for k, w in enumerate((f_wq, f_wk, f_wv)):
                sp.dma_start(w_experts[:, :, k, :], w.rearrange("e c d -> c e d")).then_inc(w_loaded, 16)
            sp.dma_start(w_experts[:, :, 3, :], f_bv.unsqueeze(0).broadcast_to([P, E, C])).then_inc(w_loaded, 16)
            with nc.allow_non_contiguous_dma(reason="biases onto partitions"):
                sp.dma_start(b_experts[:, 0, :], f_bq.rearrange("e c -> c e")).then_inc(w_loaded, 16)
                sp.dma_start(b_experts[:, 1, :], f_bk.rearrange("e c -> c e")).then_inc(w_loaded, 16)
            sp.dma_start(wg1[:, :], f_wg1).then_inc(w_loaded, 16)
            sp.dma_start(wg2[:, :], f_wg2).then_inc(w_loaded, 16)
            sp.dma_start(bg1[:, :], f_bg1.unsqueeze(1)).then_inc(w_loaded, 16)
            sp.dma_start(bg2[:, :], f_bg2.unsqueeze(0).broadcast_to([P, E])).then_inc(w_loaded, 16)
            sp.dma_start(wo[:, :], f_wo).then_inc(w_loaded, 16)
            sp.dma_start(bo[:, :], f_bo.unsqueeze(0).broadcast_to([P, C])).then_inc(w_loaded, 16)
            for h in range(2):
                sp.dma_start(wkv2[:, h, :], a_wkv).then_inc(aw_loaded, 16)
                sp.dma_start(null_col[h * AD:(h + 1) * AD, :], a_null.unsqueeze(1)).then_inc(aw_loaded, 16)
            sp.dma_start(wout[:, :, :], a_wout.rearrange("(p q) c -> q p c", q=P)).then_inc(aw_loaded, 16)
            sp.sem_inc(max_rows, 16)

            def store_parts(f, b):
                sp.wait_ge(part3_ready, 4 * f + 4)
                for k, dram in enumerate((q_parts_dram, k_parts_dram)):
                    for i in range(3):
                        sp.dma_start(dram.ap()[b * FH:(b + 1) * FH, i],
                                     parts[:, k, i, :]).then_inc(parts_stored, 16)

            def load_stacks(g, u, ul, first):
                if not first:
                    sp.wait_ge(scores_done, TB * u - TB * (NB - 1))
                qs = q_stack[0:72, g, :]
                sp.dma_start(q_stack[0:72, g, :],
                             q_parts_dram.ap()[bass.ds(ul, 1)].rearrange("u i d t -> u (i d) t").broadcast_to([3, 3 * FD, T])
                             ).then_inc(stacks_loaded[g], 16)
                for j in range(3):
                    sp.dma_start(k_stack[24 * j:24 * j + 24, g, :],
                                 k_parts_dram.ap()[bass.ds(ul, 1), j].broadcast_to([3, FD, T])).then_inc(stacks_loaded[g], 16)

            def store_o(g, u, ul):
                sp.wait_ge(o_ready, u + 1)
                for q in range(4):
                    sp.dma_start(o_dram.ap()[bass.ds(ul, 1), q], o_unit[32 * q:32 * q + 2 * FD, g % 2, :]
                                 ).then_inc(o_stored[g % 2], 16)

            def max_rows_in(g, u):
                sp.wait_ge(max_T_ready, u + 1)
                for part in range(2):
                    for blk in range(4):
                        sp.dma_start(
                            q_stack[96 + part:97 + part, g, :].rearrange("p (t b c) -> p t b c", t=NT, b=4)[:, :, blk, :],
                            max_T[32 * blk + NT * part:32 * blk + NT * part + NT, :]).then_inc(max_rows, 16)

            def ffn(ph):
                for b in range(B):
                    store_parts(ph * B + b, b)
                sp.wait_ge(parts_stored, 96 * B * (ph + 1))
                sp.wait_ge(stacks_clear, 3 * ph + 3)
                for g in range(NB):
                    load_stacks(g, ph * UNITS + g, g, ph == 0)
                max_rows_in(0, ph * UNITS)

                def body(ul, first, last):
                    for g in range(NB):
                        u = ph * UNITS + ul + g
                        if not (last and g == NB - 1):
                            max_rows_in((g + 1) % NB, u + 1)
                        if not (first and g == 0):
                            store_o((g - 1) % NB, u - 1, ul + g - 1)
                        if not last:
                            load_stacks(g, u + NB, ul + g + NB, False)
                body(0, True, False)
                with sp.Fori(1, UNITS // NB - 1) as i:
                    body(i * NB, False, False)
                body(UNITS - NB, False, True)
                store_o(NB - 1, (ph + 1) * UNITS - 1, UNITS - 1)
                for b in range(B):
                    if b == 0:
                        for par in range(2):
                            sp.wait_ge(o_stored[par], 32 * UNITS * (ph + 1))
                    sp.wait_ge(on_ready, ph * B + b)
                    for kind in range(2):
                        for g in range(4):
                            sp.dma_start(o_all[:, kind, g // 2, (g % 2) * HALF:(g % 2 + 1) * HALF],
                                         o_dram.ap()[b * FH:(b + 1) * FH, g, kind * FD:(kind + 1) * FD, :]).then_inc(o_loaded, 16)

            def load_wq(par, pg, pl):
                if not isinstance(pg, int) or pg >= 2:
                    sp.wait_ge(proj_done, 2 * pg - 2)
                sp.dma_start(wq_pair[:, par, :], a_wq[:, bass.ds(pl * 2 * AD, 2 * AD)]).then_inc(wq_loaded[par], 16)

            def build_q_s(par, pg):
                sp.wait_ge(q3_ready, 2 * pg + 2)
                if not isinstance(pg, int) or pg >= 2:
                    sp.wait_ge(a_scores, NS * pg - NS)
                for hh in range(2):
                    rows = slice(hh * AD, (hh + 1) * AD)
                    sp.dma_start(q_s[AD:P, par, hh, :, :], q_part[rows, :, :]).then_inc(q_s_loaded[par], 16)
                    sp.dma_start(q_s[0:AD, par, hh, 0:2, :], q_part[rows, 0:2, :]).then_inc(q_s_loaded[par], 16)
                    sp.dma_start(q_s[0:AD, par, hh, 2, :], q_part[rows, 0, :]).then_inc(q_s_loaded[par], 16)

            def attention(b):
                pb = b * PAIRS
                for k in range(2):
                    load_wq(k, pb + k, k)
                build_q_s(0, pb)

                def body(pl, last):
                    for k in range(2):
                        if not (last and k == 1):
                            build_q_s((k + 1) % 2, pb + pl + k + 1)
                        if not last:
                            load_wq(k, pb + pl + k + 2, pl + k + 2)
                body(0, False)
                with sp.Fori(1, PAIRS // 2 - 1) as i:
                    body(i * 2, False)
                body(PAIRS - 2, True)

            ffn(0)
            for b in range(B):
                attention(b)
            ffn(1)
            for b in range(B):
                sp.wait_ge(x_ready, 4 * B + 2 * b + 2)
                sp.dma_start(out[b].rearrange("(t p) c -> p t c", p=P), x[:, b * NT:(b + 1) * NT, :]).then_inc(out_stored, 16)
            sp.wait_ge(out_stored, 16 * B)

        @block.gpsimd
        def _(pool):
            nc.gpsimd.memset(ident[:, :], 1.0).then_inc(const_ready, 1)
            nc.gpsimd.memset(tri[:, :, :], 1.0).then_inc(const_ready, 1)
            pool.wait_ge(const_ready, 2)
            nc.gpsimd.affine_select(out=ident[:, :], in_=ident[:, :], compare_op=ALU.is_equal, fill=0.0, base=0,
                                    pattern=[[-1, P]], channel_multiplier=1).then_inc(const_ready, 1)
            nc.gpsimd.affine_select(out=tri[:, :, :], in_=tri[:, :, :], compare_op=ALU.is_ge, fill=0.0, base=-1,
                                    pattern=[[1, E], [-1, E]], channel_multiplier=0).then_inc(const_ready, 1)
            nc.gpsimd.memset(v_unit[:, :, :, :], 0.0).then_inc(const_ready, 1)
            nc.gpsimd.memset(max_parts[:, :], 0.0).then_inc(const_ready, 1)
            pool.wait_ge(const_ready, 6)
            nc.gpsimd.memset(v_unit[:, :, :, FD:2 * FD], 1.0).then_inc(const_ready, 1)
            pool.wait_ge(const_ready, 7)

            def wait(semaphore, value):
                pool.wait_ge(semaphore, value)
                pool.sem_inc(pool_waited, 1)

            nc.gpsimd.memset(causal[:, :], 0.0).then_inc(const_ready, 1)
            nc.gpsimd.tensor_copy(ident_bf[:, :], ident[:, :]).then_inc(const_ready, 1)
            nc.gpsimd.memset(null_sel[:, :], 0.0).then_inc(const_ready, 1)
            pool.wait_ge(const_ready, 10)
            nc.gpsimd.affine_select(out=causal[:, :], in_=causal[:, :], compare_op=ALU.is_ge, fill=MASKED, base=0,
                                    pattern=[[-1, P]], channel_multiplier=1).then_inc(const_ready, 1)
            pool.wait_ge(const_ready, 11)
            pool.wait_ge(aw_loaded, 16 * 5)
            for h in range(2):
                nc.gpsimd.tensor_copy(null_sel[h * AD:(h + 1) * AD, h:h + (PAIRS - 1) * (AH + 2) + 1:AH + 2],
                                      null_col[h * AD:(h + 1) * AD, :].broadcast_to([AD, PAIRS])).then_inc(const_ready, 1)
                pool.wait_ge(const_ready, 12 + h)

            def split(f):
                for c in range(4):
                    k, s = c // 2, slice((c % 2) * HALF, (c % 2 + 1) * HALF)
                    pool.wait_ge(part1_ready, 4 * f + c + 1)
                    nc.gpsimd.tensor_tensor(qkr[:, k, s], qkf[:, k, s], parts[:, k, 0, s], ALU.subtract).then_inc(rest_ready, 1)
                for c in range(4):
                    k, s = c // 2, slice((c % 2) * HALF, (c % 2 + 1) * HALF)
                    pool.wait_ge(part2_ready, 4 * f + c + 1)
                    nc.gpsimd.tensor_tensor(parts[:, k, 2, s], qkr[:, k, s], parts[:, k, 1, s], ALU.subtract).then_inc(part3_ready, 1)

            def prepare(g, u, ul, first):
                if not first:
                    wait(scores_done, TB * u - TB * (NB - 1))
                    wait(pv_done, NT // 2 * u - NT // 2 * (NB - 1))
                nc.gpsimd.memset(q_stack[96:98, g, :], 0.0).then_inc(rows_zeroed, 1)
                wait(rows_zeroed, u + 1)
                nc.gpsimd.tensor_copy(v_unit[:, g, :, 0:FD],
                                      v_all[:, bass.ds(ul, 1), :, :].rearrange("p u k d -> p (u k) d")).then_inc(v_unit_ready, 1)
                wait(v_unit_ready, u + 1)

            def clear_stacks(ph):
                if ph:
                    pool.wait_ge(x_ready, 4 * B)
                nc.gpsimd.memset(q_stack[:, :, :], 0.0).then_inc(stacks_clear, 1)
                nc.gpsimd.memset(k_stack[:, :, :], 0.0).then_inc(stacks_clear, 1)
                pool.wait_ge(stacks_clear, 3 * ph + 2)
                nc.gpsimd.memset(k_stack[96:98, :, :], 1.0).then_inc(stacks_clear, 1)
                pool.wait_ge(stacks_clear, 3 * ph + 3)

            def ffn(ph):
                clear_stacks(ph)
                for b in range(B):
                    split(ph * B + b)
                pool.wait_ge(part3_ready, 4 * B * (ph + 1))
                pool.wait_ge(v_ready, 2 * B * (ph + 1))
                for g in range(NB - 1):
                    prepare(g, ph * UNITS + g, g, ph == 0)

                def body(ul, last):
                    for g in range(NB):
                        if not last or g == 0:
                            prepare((g - 1) % NB, ph * UNITS + ul + g - 1 + NB, ul + g - 1 + NB, False)
                body(0, False)
                with pool.Fori(1, UNITS // NB - 1) as i:
                    body(i * NB, False)
                body(UNITS - NB, True)

            def q_third(pg, h):
                s = slice(h * HALF, (h + 1) * HALF)
                wait(q2_ready, 2 * pg + h + 1)
                nc.gpsimd.tensor_tensor(q_part[:, 2, s], q_rest[:, s], q_part[:, 1, s], ALU.subtract).then_inc(q3_ready, 1)
                wait(q3_ready, 2 * pg + h + 1)

            def normalize(pg, t):
                n = 1 + (STEPS[t][2] + 1) * P
                wait(a_rsum_ready, NS * pg + t + 1)
                nc.gpsimd.tensor_scalar(a_probs[:, t % RING, 1:n], a_probs[:, t % RING, 1:n], a_rsum[:, t:t + 1], 1.0,
                                        ALU.mult, ALU.mult).then_inc(a_normed, 1)
                wait(a_normed, NS * pg + t + 1)

            def attention(b):
                pb = b * PAIRS
                for h in range(2):
                    q_third(pb, h)

                def body(pl, last):
                    for k in range(2):
                        pg = pb + pl + k
                        for t in range(NS):
                            normalize(pg, t)
                            if t - 1 in Q_STEPS and not (last and k == 1):
                                q_third(pg + 1, Q_STEPS.index(t - 1))
                with pool.Fori(0, PAIRS // 2 - 1) as i:
                    body(i * 2, False)
                body(PAIRS - 2, True)

            ffn(0)
            for b in range(B):
                attention(b)
            ffn(1)

        @block.scalar
        def _(act):
            act.wait_ge(eps_ready, 1)
            act.sem_inc(probs_ready, TB)

            def norm_std(n, b):
                act.wait_ge(mv_ready, n + 1)
                nc.scalar.activation(rstd[:, b * NT:(b + 1) * NT], mean_var[:, b * NT:(b + 1) * NT, 1], ACT.Sqrt,
                                     bias=eps_col[:, 0:1]).then_inc(std_ready, 1)

            def norm_T(n, b):
                for h in range(2):
                    act.wait_ge(xT_done, 2 * n + h + 1)
                    nc.scalar.activation(xnT[:, b, h * HALF:(h + 1) * HALF], ps[:, h, :], ACT.Copy,
                                         accum_out=tok_sum[:, b, h:h + 1]).then_inc(xnT_ready, 1)

            def gates(f, b):
                act.wait_ge(hid_done, f + 1)
                nc.scalar.activation(hid[:, :], ps[:, 6, 0:1].to_broadcast([P, P]), ACT.Relu, bias=bg1[:, 0:1],
                                     scale=1.0 / T).then_inc(hid_ready, 1)
                act.wait_ge(gexp_in, f + 1)
                nc.scalar.activation(g_s[:, 1, :], g_s[:, 0, :], ACT.Exp).then_inc(gexp_out, 1)

            def split(f):
                for c in range(4):
                    k, s = c // 2, slice((c % 2) * HALF, (c % 2 + 1) * HALF)
                    act.wait_ge(qkf_ready, 4 * f + c + 1)
                    if f:
                        act.wait_ge(parts_stored, 96 * f)
                    nc.scalar.activation(parts[:, k, 0, s], qkf[:, k, s], ACT.Copy).then_inc(part1_ready, 1)
                for c in range(4):
                    k, s = c // 2, slice((c % 2) * HALF, (c % 2 + 1) * HALF)
                    act.wait_ge(rest_ready, 4 * f + c + 1)
                    nc.scalar.activation(parts[:, k, 1, s], qkr[:, k, s], ACT.Copy).then_inc(part2_ready, 1)

            def wait(semaphore, value):
                act.wait_ge(semaphore, value)
                act.sem_inc(act_waited, 1)

            def key_parts(b):
                act.wait_ge(av_done, b + 1)
                nc.scalar.activation(av[:, :, :].rearrange("p t d -> p (t d)"), ps[:, 4, :], ACT.Copy).then_inc(av_ready, 1)
                act.wait_ge(kvf_ready, b + 1)
                nc.scalar.activation(k_b[:, 0:KEYS], kvf[:, 0:KEYS], ACT.Copy).then_inc(k_split, 1)
                act.wait_ge(kvr_ready, b + 1)
                nc.scalar.activation(k_a[:, 0:KEYS], kvr[:, 0:KEYS], ACT.Copy).then_inc(k_split, 1)
                act.wait_ge(k3_ready, b + 1)
                nc.scalar.activation(k_a[0:AD, 0:KEYS], kvf[0:AD, 0:KEYS], ACT.Copy).then_inc(keys_ready, 1)

            def q_first(pg, par, h):
                if h == 0 and (not isinstance(pg, int) or pg >= 1):
                    act.wait_ge(q_s_loaded[1 - par], 48 * (pg - 1 - (1 - par)) + 96)
                act.wait_ge(proj_done, 2 * pg + h + 1)
                nc.scalar.activation(q_part[:, 0, h * HALF:(h + 1) * HALF], ps[:, PV_BANK, :], ACT.Copy,
                                     scale=A_SCALE).then_inc(q1_ready, 1)

            def q_second(pg, h, k):
                act.wait_ge(pv_bank_free, k + 1)
                nc.scalar.activation(q_part[:, 1, h * HALF:(h + 1) * HALF], q_rest[:, h * HALF:(h + 1) * HALF],
                                     ACT.Copy).then_inc(q2_ready, 1)

            def a_exps(pg, t):
                qh, hh, qt = STEPS[t]
                n = 1 + (qt + 1) * P
                act.wait_ge(a_max, NS * pg + t + 1)
                if t >= RING or not isinstance(pg, int) or pg >= 1:
                    before, pair = (t - RING, pg) if t >= RING else (NS + t - RING, pg - 1)
                    use = FIRST_USE[before] + len(USES[before]) - 1
                    act.wait_ge(tr_done[use % 2], N_USES // 2 * pair + use // 2 + 1)
                nc.scalar.activation(a_probs[:, t % RING, 0:n],
                                     ps[:, S_BANK[t % 2]:S_BANK[t % 2] + (n + HALF - 1) // HALF, :].rearrange("p a b -> p (a b)")[:, 0:n],
                                     ACT.Exp, bias=a_neg_max[:, t:t + 1], accum_out=a_sum[:, t:t + 1]).then_inc(a_exp, 1)

            def a_evac(pg, t):
                qh, hh, qt = STEPS[t]
                for k, (kt, m) in enumerate(USES[t]):
                    use = FIRST_USE[t] + k
                    if use % 2 == 1:
                        act.wait_ge(tr_done[1], N_USES // 2 * pg + use // 2 + 1)
                        nc.scalar.activation(probs_T[qh][:, hh, kt:kt + m, (qt % 4) * P:(qt % 4 + 1) * P],
                                             ps[:, T_BANK[1], 0:m * P].rearrange("p (k q) -> p k q", q=P), ACT.Copy).then_inc(evac_act, 1)

            def attention(b):
                pb = b * PAIRS
                norm_std(2 + b, b)
                norm_T(2 + b, b)
                key_parts(b)
                for h in range(2):
                    q_first(pb, 0, h)
                    q_second(pb, h, 4 * pb + h)

                def body(pl, first, last):
                    for k in range(2):
                        pg = pb + pl + k
                        for t in range(NS):
                            if t > A_LAG:
                                a_evac(pg, t - A_LAG - 1)
                            elif not (first and k == 0):
                                a_evac(pg - 1, NS + t - A_LAG - 1)
                            a_exps(pg, t)
                            if t in Q_STEPS and not (last and k == 1):
                                q_first(pg + 1, (k + 1) % 2, Q_STEPS.index(t))
                            if t - 1 in Q_STEPS and not (last and k == 1):
                                h = Q_STEPS.index(t - 1)
                                q_second(pg + 1, h, 4 * pg + 2 + h)
                body(0, True, False)
                with act.Fori(1, PAIRS // 2 - 1) as i:
                    body(i * 2, False, False)
                body(PAIRS - 2, False, True)
                for t in range(NS - A_LAG - 1, NS):
                    a_evac(pb + PAIRS - 1, t)
                for h in range(2):
                    act.wait_ge(p0T_done, 2 * b + h + 1)
                    nc.scalar.activation(p0_T[:, h * HALF:(h + 1) * HALF], ps[0:AH, 2 + h, :], ACT.Copy).then_inc(p0T_ready, 1)
                if b == 0:
                    act.wait_ge(null_done, 1)
                    nc.scalar.activation(null_out[:, :], ps[0:AH, 4, 0:C], ACT.Copy).then_inc(null_ready, 1)

            def evacuate(g, u):
                act.wait_ge(pv_done, NT // 2 * u + NT // 2)
                act.wait_ge(o_stored[g % 2], 32 * (u - g % 2))
                nc.scalar.activation(o_unit[:, g % 2, :], ps[:, PV_BANK, :], ACT.Copy).then_inc(o_ready, 1)

            def exps(g, u, first):
                for t in range(TB):
                    act.wait_ge(scores_done, TB * u + t + 1)
                    if t % 4 == 0 and not first:
                        act.wait_ge(pv_done, NT // 2 * u - NT // 2 + t // 4 + 1)
                    nc.scalar.activation(probs[:, t, :], ps[:, EXP_BANK[t], :], ACT.Exp, scale=F_SCALE).then_inc(probs_ready, 1)
                    if t == 4 and not first:
                        evacuate((g - 1) % NB, u - 1)

            def ffn(ph):
                for b in range(B):
                    norm_std(2 * ph * B + b, b)
                    norm_T(2 * ph * B + b, b)
                    gates(ph * B + b, b)
                    split(ph * B + b)

                def body(ul, first):
                    for g in range(NB):
                        exps(g, ph * UNITS + ul + g, first and g == 0)
                body(0, True)
                with act.Fori(1, UNITS // NB) as i:
                    body(i * NB, False)
                evacuate(NB - 1, ph * UNITS + UNITS - 1)

            ffn(0)
            for b in range(B):
                attention(b)
            ffn(1)

        @block.vector
        def _(dve):
            made = [0]

            def link(ins):
                made[0] += 1
                ins.then_inc(dve_link, 1)
                dve.wait_ge(dve_link, made[0])

            nc.vector.memset(eps_col[:, :], EPS).then_inc(eps_ready, 1)
            dve.sem_inc(max_read, 2)

            def norm(n, b):
                if n < B:
                    dve.wait_ge(x_loaded[b], 16)
                else:
                    dve.wait_ge(x_ready, 2 * (n - B) + 2)
                for t in range(b * NT, (b + 1) * NT):
                    ins = nc.vector.bn_stats(stats[:, t, :], x[:, t, :])
                link(ins)
                for t in range(b * NT, (b + 1) * NT):
                    ins = nc.vector.bn_aggr(mean_var[:, t, :], stats[:, t, :])
                ins.then_inc(mv_ready, 1)
                dve.wait_ge(std_ready, n + 1)
                if n:
                    dve.wait_ge(xT_done, 2 * n)
                link(nc.vector.reciprocal(rstd[:, b * NT:(b + 1) * NT], rstd[:, b * NT:(b + 1) * NT]))
                for t in range(b * NT, (b + 1) * NT):
                    ins = nc.vector.tensor_scalar(xn[:, t % NT, :], x[:, t, :], mean_var[:, t, 0:1], rstd[:, t:t + 1],
                                                  ALU.subtract, ALU.mult)
                    if t % 4 == 3:
                        ins.then_inc(xn_ready, 1)

            def gating(f, b):
                dve.wait_ge(logits_done, f + 1)
                if f == 0:
                    dve.wait_ge(w_loaded, 16 * 12)
                    dve.wait_ge(const_ready, 7)
                link(nc.vector.tensor_tensor(lg[:, :], ps[:, 6, 8:8 + E], bg2[:, :], ALU.add))
                other = lg[:, :].unsqueeze(1).broadcast_to([P, E, E])
                own = lg[:, :].unsqueeze(2).broadcast_to([P, E, E])
                nc.vector.tensor_tensor(g_cmp[:, :, :], other, own, ALU.is_gt)
                link(nc.vector.tensor_tensor(g_eq[:, :, :], other, own, ALU.is_equal))
                link(nc.vector.tensor_tensor(g_eq[:, :, :], g_eq[:, :, :], tri[:, :, :], ALU.mult))
                link(nc.vector.tensor_tensor(g_cmp[:, :, :], g_cmp[:, :, :], g_eq[:, :, :], ALU.add))
                nc.vector.reduce_sum(g_s[:, 2, :], g_cmp[:, :, :], AX)
                link(nc.vector.reduce_max(g_s[:, 3, 0:1], lg[:, :], AX))
                link(nc.vector.tensor_scalar(g_s[:, 4, :], g_s[:, 2, :], 1.5, None, ALU.is_lt))
                nc.vector.tensor_scalar(g_s[:, 0, :], lg[:, :], g_s[:, 3, 0:1], None, ALU.subtract).then_inc(gexp_in, 1)
                dve.wait_ge(gexp_out, f + 1)
                link(nc.vector.tensor_tensor(g_s[:, 5, :], g_s[:, 1, :], g_s[:, 4, :], ALU.mult))
                link(nc.vector.reduce_sum(g_s[:, 6, 0:1], g_s[:, 5, :], AX))
                link(nc.vector.reciprocal(g_s[:, 7, 0:1], g_s[:, 6, 0:1]))
                link(nc.vector.tensor_scalar(gate[:, b, :], g_s[:, 5, :], g_s[:, 7, 0:1], None, ALU.mult))
                wm = w_mix[:, b].rearrange("p k d -> p (k d)")
                bm = b_mix[:, b, :]
                for e in range(E):
                    we = w_experts[:, e].rearrange("p k d -> p (k d)")
                    be = b_experts[:, :, e]
                    ge = gate[:, b, e:e + 1]
                    if e == 0:
                        nc.vector.tensor_scalar(bm, be, ge, None, ALU.mult)
                        link(nc.vector.tensor_scalar(wm, we, ge, None, ALU.mult))
                    else:
                        nc.vector.scalar_tensor_tensor(bm, be, ge, bm, ALU.mult, ALU.add)
                        ins = nc.vector.scalar_tensor_tensor(wm, we, ge, wm, ALU.mult, ALU.add)
                        if e < E - 1:
                            link(ins)
                        else:
                            ins.then_inc(mix_ready, 1)

            def project(f, b):
                dve.wait_ge(mix_ready, f + 1)
                for c in range(4):
                    k, s = c // 2, slice((c % 2) * HALF, (c % 2 + 1) * HALF)
                    dve.wait_ge(qk_done, 4 * f + c + 1)
                    if f:
                        dve.wait_ge(rest_ready, 4 * f)
                        dve.wait_ge(part1_ready, 4 * f)
                    nc.vector.tensor_scalar(qkf[:, k, s], ps[:, 2 + c, :], b_mix[:, b, k:k + 1], None, ALU.add).then_inc(qkf_ready, 1)
                for g in range(2):
                    dve.wait_ge(vproj_done, 2 * f + g + 1)
                    for t in range(4):
                        ins = nc.vector.tensor_tensor(
                            v_all[:, b * FH:(b + 1) * FH, 4 * g + t, :],
                            ps[:, 6 + g, t * C:(t + 1) * C].rearrange("p (h d) -> p h d", d=FD),
                            w_mix[:, b, 3, :].rearrange("p (h d) -> p h d", d=FD), ALU.add)
                    ins.then_inc(v_ready, 1)

            def maxima(g, u):
                for t in range(NT):
                    dve.wait_ge(max_scores, NT * u + t + 1)
                    bank = MAX_BANK[t % 2]
                    nc.vector.tensor_reduce(neg_max[:, g, t:t + 1], ps[:, bank:bank + 2, :].rearrange("p a b -> p (a b)"), AX,
                                            ALU.max, negate=True).then_inc(max_read, 1)
                dve.wait_ge(max_read, 2 + NT * u + NT)
                nc.vector.tensor_copy(max_parts[:, 0:NT], neg_max[:, g, :]).then_inc(max_link, 1)
                dve.wait_ge(max_link, 2 * u + 1)
                nc.vector.tensor_tensor(max_parts[:, NT:2 * NT], neg_max[:, g, :], max_parts[:, 0:NT], ALU.subtract).then_inc(max_link, 1)
                dve.wait_ge(max_link, 2 * u + 2)
                dve.wait_ge(max_rows, 128 * u + 16)
                nc.vector.transpose(max_T[:, :], max_parts[:, :]).then_inc(max_T_ready, 1)

            def finish(f, b):
                dve.wait_ge(o_loaded, 128 * (f + 1))
                nc.vector.tensor_tensor(num[:, :], o_all[:, 0, 0, :], o_all[:, 0, 1, :], ALU.add)
                link(nc.vector.tensor_tensor(den[:, :], o_all[:, 1, 0, :], o_all[:, 1, 1, :], ALU.add))
                link(nc.vector.reciprocal(den[:, :], den[:, :]))
                nc.vector.tensor_tensor(num[:, :], num[:, :], den[:, :], ALU.mult).then_inc(on_ready, 1)
                for g in range(2):
                    xs = x[:, b * NT + 4 * g:b * NT + 4 * g + 4, :]
                    dve.wait_ge(y_done, 2 * f + g + 1)
                    n = f if f < B else f + B
                    dve.wait_ge(x_ready, 2 * n + g)
                    nc.vector.tensor_tensor(ytmp[:, :, :], ps[:, g, :].rearrange("p (t c) -> p t c", c=C),
                                            bo[:, :].unsqueeze(1).broadcast_to([P, 4, C]), ALU.add).then_inc(dve_link, 1)
                    made[0] += 1
                    dve.wait_ge(dve_link, made[0])
                    nc.vector.scalar_tensor_tensor(xs, ytmp[:, :, :], 0.5, xs, ALU.mult, ALU.add).then_inc(x_ready, 1)

            def keys(b):
                if b:
                    dve.wait_ge(x_ready, 2 * B + 2 * b)
                for h in range(2):
                    dve.wait_ge(kv_done, 2 * b + h + 1)
                    ins = nc.vector.tensor_copy(kvf[:, 1 + h * HALF:1 + (h + 1) * HALF], ps[:, 2 + h, :])
                nc.vector.tensor_copy(kvf[:, 0:1], null_col[:, :]).then_inc(kvf_ready, 1)
                dve.wait_ge(k_split, 2 * b + 1)
                nc.vector.tensor_tensor(kvr[:, 0:KEYS], kvf[:, 0:KEYS], k_b[:, 0:KEYS], ALU.subtract).then_inc(kvr_ready, 1)
                dve.wait_ge(k_split, 2 * b + 2)
                nc.vector.tensor_tensor(k_b[0:AD, 0:KEYS], kvr[0:AD, 0:KEYS], k_a[0:AD, 0:KEYS], ALU.subtract).then_inc(k3_ready, 1)

            def q_rests(pg, h):
                if h == 0 and (not isinstance(pg, int) or pg >= 1):
                    dve.wait_ge(q3_ready, 2 * pg)
                dve.wait_ge(q1_ready, 2 * pg + h + 1)
                s = slice(h * HALF, (h + 1) * HALF)
                nc.vector.scalar_tensor_tensor(q_rest[:, s], ps[:, PV_BANK, :], A_SCALE, q_part[:, 0, s], ALU.mult,
                                               ALU.subtract).then_inc(pv_bank_free, 1)

            def a_maximum(pg, t):
                n = 1 + (STEPS[t][2] + 1) * P
                dve.wait_ge(a_scores, NS * pg + t + 1)
                nc.vector.tensor_reduce(a_neg_max[:, t:t + 1],
                                        ps[:, S_BANK[t % 2]:S_BANK[t % 2] + (n + HALF - 1) // HALF, :].rearrange("p a b -> p (a b)")[:, 0:n],
                                        AX, ALU.max, negate=True).then_inc(a_max, 1)

            def a_recip(pg, pl, t):
                qh, hh, qt = STEPS[t]
                dve.wait_ge(a_exp, NS * pg + t + 1)
                nc.vector.reciprocal(a_rsum[:, t:t + 1], a_sum[:, t:t + 1]).then_inc(a_rsum_ready, 1)
                dve.wait_ge(a_rsum_ready, NS * pg + t + 1)
                nc.vector.tensor_tensor(p0[:, qt, bass.ds(2 * pl + hh, 1)], a_probs[:, t % RING, 0:1], a_rsum[:, t:t + 1],
                                        ALU.mult).then_inc(p0_ready, 1)

            def a_evac(pg, t):
                qh, hh, qt = STEPS[t]
                for k, (kt, m) in enumerate(USES[t]):
                    use = FIRST_USE[t] + k
                    if use % 2 == 0:
                        dve.wait_ge(tr_done[0], N_USES // 2 * pg + use // 2 + 1)
                        nc.vector.tensor_copy(probs_T[qh][:, hh, kt:kt + m, (qt % 4) * P:(qt % 4 + 1) * P],
                                              ps[:, T_BANK[0], 0:m * P].rearrange("p (k q) -> p k q", q=P)).then_inc(evac_dve, 1)

            def o_evac(pg, pl, qh):
                dve.wait_ge(apv_done, 2 * pg + qh + 1)
                nc.vector.tensor_scalar(o_T[:, bass.ds(pl, 1), qh * HALF:(qh + 1) * HALF].rearrange("p a b -> p (a b)"),
                                        ps[:, PV_BANK, :], 1.0, None, ALU.mult).then_inc(pv_bank_free, 1)

            def attention(b):
                pb = b * PAIRS
                norm(2 + b, b)
                keys(b)
                for h in range(2):
                    q_rests(pb, h)

                def body(pl, first, last):
                    for k in range(2):
                        pg = pb + pl + k
                        for t in range(NS):
                            if t > A_LAG:
                                a_evac(pg, t - A_LAG - 1)
                            elif not (first and k == 0):
                                a_evac(pg - 1, NS + t - A_LAG - 1)
                            if t >= 2:
                                a_recip(pg, pl + k, t - 2)
                            elif not (first and k == 0):
                                a_recip(pg - 1, pl + k - 1, NS + t - 2)
                            a_maximum(pg, t)
                            if t == A_LAG + 1 and not (first and k == 0):
                                o_evac(pg - 1, pl + k - 1, 1)
                            if t in Q_STEPS and not (last and k == 1):
                                q_rests(pg + 1, Q_STEPS.index(t))
                            if t == 9 + A_LAG:
                                o_evac(pg, pl + k, 0)
                body(0, True, False)
                with dve.Fori(1, PAIRS // 2 - 1) as i:
                    body(i * 2, False, False)
                body(PAIRS - 2, False, True)
                for t in range(NS - 2, NS):
                    a_recip(pb + PAIRS - 1, PAIRS - 1, t)
                for t in range(NS - A_LAG - 1, NS):
                    a_evac(pb + PAIRS - 1, t)
                o_evac(pb + PAIRS - 1, PAIRS - 1, 1)
                for g in range(2):
                    dve.wait_ge(ay_done, 2 * b + g + 1)
                    xs = x[:, b * NT + 4 * g:b * NT + 4 * g + 4, :].rearrange("p t c -> p (t c)")
                    nc.vector.tensor_tensor(xs, ps[:, g, :], xs, ALU.add).then_inc(x_ready, 1)

            def ffn(ph):
                for b in range(B):
                    norm(2 * ph * B + b, b)
                    gating(ph * B + b, b)
                    project(ph * B + b, b)
                with dve.Fori(0, UNITS // NB) as i:
                    for g in range(NB):
                        maxima(g, ph * UNITS + i * NB + g)
                for b in range(B):
                    finish(ph * B + b, b)

            ffn(0)
            for b in range(B):
                attention(b)
            ffn(1)

        @block.tensor
        def _(pe):
            pe.wait_ge(const_ready, 7)
            pe.wait_ge(w_loaded, 16 * 12)

            def norm_T(n, b):
                for h in range(2):
                    pe.wait_ge(xn_ready, 2 * n + h + 1)
                    for t in range(4):
                        ins = nc.tensor.transpose(ps[:, h, t * P:(t + 1) * P], xn[:, 4 * h + t, :], ident[:, :])
                    ins.then_inc(xT_done, 1)

            def gates(n, f, b):
                pe.wait_ge(xnT_ready, 2 * n + 2)
                for h in range(2):
                    ins = nc.tensor.matmul(ps[:, 6, 0:1], wg1[:, :], tok_sum[:, b, h:h + 1], start=h == 0, stop=h == 1)
                ins.then_inc(hid_done, 1)
                pe.wait_ge(hid_ready, f + 1)
                nc.tensor.matmul(ps[:, 6, 8:8 + E], hid[:, :], wg2[:, :], start=True, stop=True).then_inc(logits_done, 1)

            def project(f, b):
                pe.wait_ge(mix_ready, f + 1)
                if f:
                    pe.wait_ge(qkf_ready, 4 * f)
                    pe.wait_ge(v_ready, 2 * f)
                for c in range(4):
                    nc.tensor.matmul(ps[:, 2 + c, :], w_mix[:, b, c // 2, :], xnT[:, b, (c % 2) * HALF:(c % 2 + 1) * HALF],
                                     start=True, stop=True).then_inc(qk_done, 1)
                for g in range(2):
                    for t in range(4):
                        ins = nc.tensor.matmul(ps[:, 6 + g, t * C:(t + 1) * C], xnT[:, b, (4 * g + t) * P:(4 * g + t + 1) * P],
                                               w_mix[:, b, 2, :], start=True, stop=True)
                    ins.then_inc(vproj_done, 1)

            def max_tile(g, u, t):
                if t == 0:
                    pe.wait_ge(stacks_loaded[g], 64 // NB * (u - g) + 64)
                    pe.wait_ge(rows_zeroed, u + 1)
                pe.wait_ge(max_read, NT * u + t + 1)
                bank = MAX_BANK[t % 2]
                for h in range(2):
                    ins = nc.tensor.matmul(ps[:, bank + h, :], q_stack[:, g, t * P:(t + 1) * P],
                                           k_stack[:, g, h * HALF:(h + 1) * HALF], start=True, stop=True)
                ins.then_inc(max_scores, 1)

            def score_tile(g, u, kt, h):
                if kt == 0 and h == 0:
                    pe.wait_ge(max_rows, 128 * u + 128 + 16)
                t = 2 * kt + h
                bank = EXP_BANK[t]
                before = max([s for s in range(t) if EXP_BANK[s] == bank] + [max(s for s in range(TB) if EXP_BANK[s] == bank) - TB
                                                                             if t < 3 else -TB])
                pe.wait_ge(probs_ready, TB + TB * u + before + 1)
                ins = nc.tensor.matmul(ps[:, bank, :], k_stack[:, g, kt * P:(kt + 1) * P],
                                       q_stack[:, g, h * HALF:(h + 1) * HALF], start=True, stop=True)
                ins.then_inc(scores_done, 1)

            def values(g, u, j):
                if j == 0:
                    pe.wait_ge(v_unit_ready, u + 1)
                    pe.wait_ge(o_ready, u)
                pe.wait_ge(probs_ready, TB + TB * u + 4 * j + 4)
                for t in range(4 * j, 4 * j + 4):
                    col = 32 * (t % 4)
                    ins = nc.tensor.matmul(ps[col:col + 32, PV_BANK, :], v_unit[:, g, t // 2, :], probs[:, t, :],
                                           start=j == 0, stop=j == NT // 2 - 1)
                ins.then_inc(pv_done, 1)

            LAG = 2

            def unit(g, u, first, ahead):
                for kt in range(NT):
                    score_tile(g, u, kt, 0)
                    if kt < NT - SHIFT and ahead > 0:
                        max_tile((g + 1) % NB, u + 1, SHIFT + kt)
                    elif kt >= NT - SHIFT and ahead > 1:
                        max_tile((g + 2) % NB, u + 2, kt - (NT - SHIFT))
                    score_tile(g, u, kt, 1)
                    if kt % 2 == 1:
                        j = kt // 2 - 1
                        if j >= 0:
                            values(g, u, j)
                        elif not first:
                            values((g - 1) % NB, u - 1, NT // 2 - 1)

            def finish(f, b):
                pe.wait_ge(on_ready, f + 1)
                for g in range(2):
                    for t in range(4):
                        ins = nc.tensor.matmul(ps[:, g, t * C:(t + 1) * C], num[:, (4 * g + t) * P:(4 * g + t + 1) * P],
                                               wo[:, :], start=True, stop=True)
                    ins.then_inc(y_done, 1)

            def keys(b):
                pe.wait_ge(xnT_ready, 2 * (2 + b) + 2)
                for h in range(2):
                    nc.tensor.matmul(ps[:, 2 + h, :], wkv2[:, :, :].rearrange("p a b -> p (a b)"), xnT[:, b, h * HALF:(h + 1) * HALF],
                                     start=True, stop=True).then_inc(kv_done, 1)
                for t in range(NT):
                    ins = nc.tensor.matmul(ps[:, 4, t * AD:(t + 1) * AD], xnT[:, b, t * P:(t + 1) * P], wkv2[:, 0, :],
                                           start=True, stop=True)
                ins.then_inc(av_done, 1)

            def queries(pg, k, b, par, h):
                if h == 0:
                    pe.wait_ge(wq_loaded[par], 8 * (pg - par) + 16)
                if not isinstance(pg, int) or k > 0:
                    pe.wait_ge(pv_bank_free, k)
                nc.tensor.matmul(ps[:, PV_BANK, :], wq_pair[:, par, :], xnT[:, b, h * HALF:(h + 1) * HALF],
                                 start=True, stop=True).then_inc(proj_done, 1)

            def a_score_tile(pg, par, t):
                qh, hh, qt = STEPS[t]
                n = 1 + (qt + 1) * P
                if t == 0:
                    pe.wait_ge(q_s_loaded[par], 48 * (pg - par) + 96)
                if t >= 2 or not isinstance(pg, int) or pg >= 1:
                    pe.wait_ge(a_exp, NS * pg + t - 1)
                cols = slice(qt * P, (qt + 1) * P)
                for c0 in range(0, n, HALF):
                    c1 = min(n, c0 + HALF)
                    m0, m1 = max(c0, 1 + qt * P), c1
                    bank = S_BANK[t % 2] + c0 // HALF
                    passes = [(q_s[:, par, hh, k, cols], key[:, c0:c1], 0, c1 - c0) for k, key in enumerate((k_a, k_a, k_b))]
                    if m1 > m0:
                        passes.append((ident_bf[:, :], causal[:, m0 - 1 - qt * P:m1 - 1 - qt * P], m0 - c0, m1 - c0))
                    for k, (lhs, rhs, o0, o1) in enumerate(passes):
                        ins = nc.tensor.matmul(ps[:, bank, o0:o1], lhs, rhs, start=k == 0, stop=k == len(passes) - 1)
                ins.then_inc(a_scores, 1)

            def a_transposes(pg, t):
                qh, hh, qt = STEPS[t]
                pe.wait_ge(a_normed, NS * pg + t + 1)
                for k, (kt, m) in enumerate(USES[t]):
                    use = FIRST_USE[t] + k
                    if use >= 2 or not isinstance(pg, int) or pg >= 1:
                        pe.wait_ge(evac_act if use % 2 else evac_dve, N_USES // 2 * pg + use // 2)
                    for j in range(m):
                        ins = nc.tensor.transpose(ps[:, T_BANK[use % 2], j * P:(j + 1) * P],
                                                  a_probs[:, t % RING, 1 + (kt + j) * P:1 + (kt + j + 1) * P], ident[:, :])
                    ins.then_inc(tr_done[use % 2], 1)

            def a_values(pg, qh, k0):
                last = [s for s in range(NS) if STEPS[s][0] == qh][-1]
                done = (FIRST_USE[last] + len(USES[last])) // 2
                pe.wait_ge(evac_dve, N_USES // 2 * pg + done)
                pe.wait_ge(evac_act, N_USES // 2 * pg + done)
                pe.wait_ge(pv_bank_free, k0)
                nk = 4 * (qh + 1)
                for kt in range(nk):
                    q0 = max(0, kt - 4 * qh) * P
                    for hh in range(2):
                        ins = nc.tensor.matmul(ps[hh * AD:(hh + 1) * AD, PV_BANK, q0:HALF], av[:, kt, :],
                                               probs_T[qh][:, hh, kt, q0:HALF], start=kt == 0, stop=kt == nk - 1)
                ins.then_inc(apv_done, 1)

            def attention(b):
                pb = b * PAIRS
                norm_T(2 + b, b)
                keys(b)
                for h in range(2):
                    queries(pb, 4 * pb + h, b, 0, h)
                pe.wait_ge(keys_ready, b + 1)
                pe.wait_ge(av_ready, b + 1)

                def body(pl, first, last):
                    for k in range(2):
                        pg = pb + pl + k
                        for t in range(NS):
                            a_score_tile(pg, k, t)
                            if t >= A_LAG:
                                a_transposes(pg, t - A_LAG)
                            elif not (first and k == 0):
                                a_transposes(pg - 1, NS + t - A_LAG)
                            if t == A_LAG and not (first and k == 0):
                                a_values(pg - 1, 1, 4 * (pg - 1) + 5)
                            if t in Q_STEPS and not (last and k == 1):
                                h = Q_STEPS.index(t)
                                queries(pg + 1, 4 * pg + 2 + h, b, (k + 1) % 2, h)
                            if t == 8 + A_LAG:
                                a_values(pg, 0, 4 * pg + (2 if last and k == 1 else 4))
                body(0, True, False)
                with pe.Fori(1, PAIRS // 2 - 1) as i:
                    body(i * 2, False, False)
                body(PAIRS - 2, False, True)
                pg = pb + PAIRS - 1
                for t in range(NS - A_LAG, NS):
                    a_transposes(pg, t)
                a_values(pg, 1, 4 * pg + 3)
                pe.wait_ge(p0_ready, NS * (pg + 1))
                pe.wait_ge(a_exp, NS * (pg + 1))
                for h in range(2):
                    for t in range(4):
                        ins = nc.tensor.transpose(ps[0:AH, 2 + h, t * P:(t + 1) * P], p0[:, 4 * h + t, :], ident[:, :])
                    ins.then_inc(p0T_done, 1)
                if b == 0:
                    pe.wait_ge(const_ready, 13)
                    for p in range(PAIRS):
                        ins = nc.tensor.matmul(ps[0:AH, 4, 0:C], null_sel[:, p * AH:(p + 1) * AH], wout[:, p, :],
                                               start=p == 0, stop=p == PAIRS - 1)
                    ins.then_inc(null_done, 1)
                    pe.wait_ge(null_ready, 1)
                pe.wait_ge(p0T_ready, 2 * b + 2)
                pe.wait_ge(pv_bank_free, 4 * (pg + 1))
                for g in range(2):
                    for t in range(4):
                        tok = slice((4 * g + t) * P, (4 * g + t + 1) * P)
                        for p in range(PAIRS):
                            nc.tensor.matmul(ps[:, g, t * C:(t + 1) * C], o_T[:, p, tok], wout[:, p, :], start=p == 0, stop=False)
                        ins = nc.tensor.matmul(ps[:, g, t * C:(t + 1) * C], p0_T[:, tok], null_out[:, :], start=False, stop=True)
                    ins.then_inc(ay_done, 1)

            def ffn(ph):
                for b in range(B):
                    norm_T(2 * ph * B + b, b)
                    gates(2 * ph * B + b, ph * B + b, b)
                    project(ph * B + b, b)
                pe.wait_ge(qkf_ready, 4 * B * (ph + 1))
                pe.wait_ge(v_ready, 2 * B * (ph + 1))
                u0 = ph * UNITS
                for t in range(NT):
                    max_tile(0, u0, t)
                for t in range(SHIFT):
                    max_tile(1, u0 + 1, t)
                for g in range(NB):
                    unit(g, u0 + g, g == 0, NB)
                with pe.Fori(1, UNITS // NB - 1) as i:
                    for g in range(NB):
                        unit(g, i * NB + (u0 + g), False, NB)
                for g in range(NB):
                    unit(g, u0 + UNITS - NB + g, False, NB - 1 - g)
                values(NB - 1, u0 + UNITS - 1, NT // 2 - 1)
                for b in range(B):
                    finish(ph * B + b, b)

            ffn(0)
            for b in range(B):
                attention(b)
            ffn(1)


_INS = ["L0_attn_x", "L0_attn_Wq", "L0_attn_Wkv", "L0_attn_null_kv", "L0_attn_Wout", "L0_ffn_Wq", "L0_ffn_bq", "L0_ffn_Wk",
        "L0_ffn_bk", "L0_ffn_Wv", "L0_ffn_bv", "L0_ffn_Wg1", "L0_ffn_bg1", "L0_ffn_Wg2", "L0_ffn_bg2", "L0_ffn_Wo", "L0_ffn_bo"]


def kernel(**inputs):
    import numpy as _np
    import concourse.bacc as _bacc
    from concourse import mybir as _mybir
    from concourse.bass_utils import run_bass_kernel_spmd as _run

    nc = _bacc.Bacc("TRN2", target_bir_lowering=False, num_devices=1)
    arrays, args = {}, []
    for name in _INS:
        a = _np.ascontiguousarray(inputs[name])
        arrays[f"in_{name}"] = a
        args.append(nc.dram_tensor(f"in_{name}", a.shape, _mybir.dt.from_np(a.dtype), kind="ExternalInput").ap())
    x_shape = inputs["L0_attn_x"].shape
    args.append(nc.dram_tensor("out_0", x_shape, _mybir.dt.float32, kind="ExternalOutput").ap())
    build(nc, *args)
    r = _run(nc, [arrays], core_ids=[0])
    return r.results[0]["out_0"]
```

```python
from contextlib import ExitStack

import concourse.bass as bass
from concourse import mybir

F32 = mybir.dt.float32
BF16 = mybir.dt.bfloat16
ALU = mybir.AluOpType
ACT = mybir.ActivationFunctionType
AX = mybir.AxisListType.X

P = 128
C = 128
EPS = 1e-5


def build(nc, x_in, a_wq, a_wkv, a_null, a_wout, f_wq, f_bq, f_wk, f_bk, f_wv, f_bv,
          f_wg1, f_bg1, f_wg2, f_bg2, f_wo, f_bo, out):
    B, T, _ = x_in.shape
    NT = T // P
    HALF = 512
    E = f_wq.shape[0]
    FH = 16
    FD = C // FH
    F_SCALE = float(FD) ** -0.5
    UNITS = B * FH
    NB = 4
    SHIFT = 7
    AH, AD = 16, a_wkv.shape[1]
    PAIRS = AH // 2
    A_SCALE = float(AD) ** -0.5
    KEYS = T + 1
    RING = 8
    A_LAG = 4
    MASKED = -1e30

    with ExitStack() as ctx:
        def sb(name, shape, dt=F32):
            return ctx.enter_context(nc.sbuf_tensor(name, shape, dt))

        def sem(name):
            return ctx.enter_context(nc.semaphore(name))

        q_parts_dram = nc.dram_tensor("q_parts_dram", [UNITS, 3, FD, T], BF16)
        k_parts_dram = nc.dram_tensor("k_parts_dram", [UNITS, 3, FD, T], BF16)
        o_dram = nc.dram_tensor("o_dram", [UNITS, 4, 2 * FD, HALF], F32)

        x = sb("x", [P, B * NT, C])
        xn = sb("xn", [P, NT, C])
        xnT = sb("xnT", [P, B, T])
        stats = sb("stats", [P, B * NT, 6])
        mean_var = sb("mean_var", [P, B * NT, 2])
        rstd = sb("rstd", [P, B * NT])
        ident = sb("ident", [P, P])
        eps_col = sb("eps_col", [P, 1])

        w_experts = sb("w_experts", [P, E, 4, C])
        w_mix = sb("w_mix", [P, B, 4, C])
        b_experts = sb("b_experts", [P, 2, E])
        b_mix = sb("b_mix", [P, B, 2])
        wg1 = sb("wg1", [P, C])
        wg2 = sb("wg2", [P, E])
        bg1 = sb("bg1", [P, 1])
        bg2 = sb("bg2", [P, E])
        wo = sb("wo", [P, C])
        bo = sb("bo", [P, C])
        tok_sum = sb("tok_sum", [P, B, 2])
        hid = sb("hid", [P, P])
        tri = sb("tri", [P, E, E])
        lg = sb("lg", [P, E])
        g_cmp = sb("g_cmp", [P, E, E])
        g_eq = sb("g_eq", [P, E, E])
        g_s = sb("g_s", [P, 8, E])
        gate = sb("gate", [P, B, E])

        neg_max = sb("neg_max", [P, NB, NT])
        max_parts = sb("max_parts", [P, 32], BF16)
        max_T = sb("max_T", [P, 32], BF16)

        wkv2 = sb("wkv2", [P, 2, AD])
        wout = sb("wout", [P, PAIRS, C])
        null_col = sb("null_col", [P, 1])
        null_sel = sb("null_sel", [P, PAIRS * AH])
        null_out = sb("null_out", [AH, C])
        ident_bf = sb("ident_bf", [P, P], BF16)
        causal = sb("causal", [P, P], BF16)
        wq_pair = sb("wq_pair", [P, 2, 2 * AD])
        a_neg_max = sb("a_neg_max", [P, 2 * NT])
        a_sum = sb("a_sum", [P, 2 * NT])
        a_rsum = sb("a_rsum", [P, 2 * NT])
        p0 = sb("p0", [P, B, NT, AH])
        p0_T = sb("p0_T", [AH, T])

        ARENA = 159 * 256 + 128
        arena = sb("arena", [P, ARENA])
        at = [0]

        def carve(shape, dt=F32, pattern=None, **dims):
            n = 1
            for k in shape:
                n *= k
            words = n if dt == F32 else (n + 1) // 2
            flat = arena[:, at[0]:at[0] + words]
            at[0] += words
            assert at[0] <= ARENA, at[0]
            if dt != F32:
                flat = flat.bitcast(dt)[:, 0:n]
            if len(shape) == 1:
                return flat
            names = "abcdef"[:len(shape)]
            return flat.rearrange(f"p ({' '.join(names)}) -> p {' '.join(names)}", **dict(zip(names, shape)))

        qkf = carve([2, T])
        qkr = carve([2, T])
        parts = carve([2, 3, T], BF16)
        v_all = carve([UNITS, NT, FD])
        probs = carve([2 * NT, HALF])
        o_unit = carve([2, HALF])
        o_all = carve([2, 2, T])
        num = carve([T])
        den = carve([T])
        q_stack = carve([NB, T], BF16)
        k_stack = carve([NB, T], BF16)
        v_unit = carve([NB, NT, 32])
        ytmp = carve([4, C])
        at[0] = 0
        k_a = carve([B, KEYS + 1], BF16)
        k_b = carve([B, KEYS + 1], BF16)
        av = carve([B, NT, AD])
        q_part = carve([3, T], BF16)
        q_rest = carve([T])
        q_s = carve([2, 2, 3, T], BF16)
        a_probs = carve([RING, KEYS + 3])
        probs_T = [carve([2, 4 * (qh + 1), HALF]) for qh in range(2)]
        o_T = carve([PAIRS, T])
        at[0] -= PAIRS * T
        kvf = carve([KEYS + 1])
        kvr = carve([KEYS + 1])

        ps = ctx.enter_context(nc.psum_tensor("ps", [P, 8, HALF], F32))
        EXP_BANK = [0, 1, 2] * 5 + [1]
        MAX_BANK = [3, 5]
        PV_BANK = 7
        S_BANK = [3, 0]
        T_BANK = [5, 6]

        w_loaded = sem("w_loaded")
        aw_loaded = sem("aw_loaded")
        wq_loaded = [sem(f"wq_loaded_{k}") for k in range(2)]
        act_waited = sem("act_waited")
        kv_done = sem("kv_done")
        av_done = sem("av_done")
        av_ready = sem("av_ready")
        kvf_ready = sem("kvf_ready")
        kvr_ready = sem("kvr_ready")
        k_split = sem("k_split")
        k3_ready = sem("k3_ready")
        keys_ready = sem("keys_ready")
        proj_done = sem("proj_done")
        q1_ready = sem("q1_ready")
        q2_ready = sem("q2_ready")
        q3_ready = sem("q3_ready")
        pv_bank_free = sem("pv_bank_free")
        q_s_loaded = [sem(f"q_s_loaded_{k}") for k in range(2)]
        a_scores = sem("a_scores")
        a_max = sem("a_max")
        a_exp = sem("a_exp")
        a_rsum_ready = sem("a_rsum_ready")
        p0_ready = sem("p0_ready")
        a_normed = sem("a_normed")
        tr_done = [sem(f"tr_done_{k}") for k in range(2)]
        evac_dve = sem("evac_dve")
        evac_act = sem("evac_act")
        apv_done = sem("apv_done")
        p0T_done = sem("p0T_done")
        p0T_ready = sem("p0T_ready")
        null_done = sem("null_done")
        null_ready = sem("null_ready")
        ay_done = sem("ay_done")
        x_loaded = [sem(f"x_loaded_{b}") for b in range(B)]
        const_ready = sem("const_ready")
        eps_ready = sem("eps_ready")
        dve_link = sem("dve_link")
        mv_ready = sem("mv_ready")
        std_ready = sem("std_ready")
        xn_ready = sem("xn_ready")
        xT_done = sem("xT_done")
        xnT_ready = sem("xnT_ready")
        hid_done = sem("hid_done")
        hid_ready = sem("hid_ready")
        logits_done = sem("logits_done")
        gexp_in = sem("gexp_in")
        gexp_out = sem("gexp_out")
        mix_ready = sem("mix_ready")
        qk_done = sem("qk_done")
        vproj_done = sem("vproj_done")
        qkf_ready = sem("qkf_ready")
        v_ready = sem("v_ready")
        part1_ready = sem("part1_ready")
        rest_ready = sem("rest_ready")
        part2_ready = sem("part2_ready")
        part3_ready = sem("part3_ready")
        parts_stored = sem("parts_stored")
        pool_waited = sem("pool_waited")
        stacks_loaded = [sem(f"stacks_loaded_{g}") for g in range(NB)]
        rows_zeroed = sem("rows_zeroed")
        stacks_clear = sem("stacks_clear")
        v_unit_ready = sem("v_unit_ready")
        max_scores = sem("max_scores")
        max_read = sem("max_read")
        max_T_ready = sem("max_T_ready")
        max_link = sem("max_link")
        max_rows = sem("max_rows")
        scores_done = sem("scores_done")
        probs_ready = sem("probs_ready")
        pv_done = sem("pv_done")
        o_ready = sem("o_ready")
        o_stored = [sem(f"o_stored_{g}") for g in range(2)]
        o_loaded = sem("o_loaded")
        on_ready = sem("on_ready")
        y_done = sem("y_done")
        x_ready = sem("x_ready")
        out_stored = sem("out_stored")

        N_W = 14
        STEPS = [(qh, hh, 4 * qh + k) for qh in range(2) for hh in range(2) for k in range(4)]
        NS = len(STEPS)
        USES = [[(k, min(4, qt + 1 - k)) for k in range(0, qt + 1, 4)] for _, _, qt in STEPS]
        FIRST_USE = [sum(len(USES[s]) for s in range(t)) for t in range(NS)]
        Q_STEPS = (A_LAG + 2, A_LAG + 4)
        P0_STEPS = (A_LAG + 2, A_LAG + 3)
        Y_STEPS = (A_LAG + 4, A_LAG + 5)
        LATE_Q_STEPS = (A_LAG + 6, A_LAG + 7)
        N_USES = sum(len(v) for v in USES)

        TB = 2 * NT

        block = ctx.enter_context(nc.Block())

        @block.sync
        def _(sp):
            for b in range(B):
                sp.dma_start(x[:, b * NT:(b + 1) * NT, :], x_in[b].rearrange("(t p) c -> p t c", p=P)).then_inc(x_loaded[b], 16)
            for k, w in enumerate((f_wq, f_wk, f_wv)):
                sp.dma_start(w_experts[:, :, k, :], w.rearrange("e c d -> c e d")).then_inc(w_loaded, 16)
            sp.dma_start(w_experts[:, :, 3, :], f_bv.unsqueeze(0).broadcast_to([P, E, C])).then_inc(w_loaded, 16)
            with nc.allow_non_contiguous_dma(reason="biases onto partitions"):
                sp.dma_start(b_experts[:, 0, :], f_bq.rearrange("e c -> c e")).then_inc(w_loaded, 16)
                sp.dma_start(b_experts[:, 1, :], f_bk.rearrange("e c -> c e")).then_inc(w_loaded, 16)
            sp.dma_start(wg1[:, :], f_wg1).then_inc(w_loaded, 16)
            sp.dma_start(wg2[:, :], f_wg2).then_inc(w_loaded, 16)
            sp.dma_start(bg1[:, :], f_bg1.unsqueeze(1)).then_inc(w_loaded, 16)
            sp.dma_start(bg2[:, :], f_bg2.unsqueeze(0).broadcast_to([P, E])).then_inc(w_loaded, 16)
            sp.dma_start(wo[:, :], f_wo).then_inc(w_loaded, 16)
            sp.dma_start(bo[:, :], f_bo.unsqueeze(0).broadcast_to([P, C])).then_inc(w_loaded, 16)
            for h in range(2):
                sp.dma_start(wkv2[:, h, :], a_wkv).then_inc(aw_loaded, 16)
                sp.dma_start(null_col[h * AD:(h + 1) * AD, :], a_null.unsqueeze(1)).then_inc(aw_loaded, 16)
            sp.dma_start(wout[:, :, :], a_wout.rearrange("(p q) c -> q p c", q=P)).then_inc(aw_loaded, 16)
            sp.sem_inc(max_rows, 16)

            def store_parts(f, b):
                sp.wait_ge(part3_ready, 4 * f + 4)
                for k, dram in enumerate((q_parts_dram, k_parts_dram)):
                    for i in range(3):
                        sp.dma_start(dram.ap()[b * FH:(b + 1) * FH, i],
                                     parts[:, k, i, :]).then_inc(parts_stored, 16)

            def load_stacks(g, u, ul, first):
                if not first:
                    sp.wait_ge(scores_done, TB * u - TB * (NB - 1))
                qs = q_stack[0:72, g, :]
                sp.dma_start(q_stack[0:72, g, :],
                             q_parts_dram.ap()[bass.ds(ul, 1)].rearrange("u i d t -> u (i d) t").broadcast_to([3, 3 * FD, T])
                             ).then_inc(stacks_loaded[g], 16)
                for j in range(3):
                    sp.dma_start(k_stack[24 * j:24 * j + 24, g, :],
                                 k_parts_dram.ap()[bass.ds(ul, 1), j].broadcast_to([3, FD, T])).then_inc(stacks_loaded[g], 16)

            def store_o(g, u, ul):
                sp.wait_ge(o_ready, u + 1)
                for q in range(4):
                    sp.dma_start(o_dram.ap()[bass.ds(ul, 1), q], o_unit[32 * q:32 * q + 2 * FD, g % 2, :]
                                 ).then_inc(o_stored[g % 2], 16)

            def max_rows_in(g, u):
                sp.wait_ge(max_T_ready, u + 1)
                for part in range(2):
                    for blk in range(4):
                        sp.dma_start(
                            q_stack[96 + part:97 + part, g, :].rearrange("p (t b c) -> p t b c", t=NT, b=4)[:, :, blk, :],
                            max_T[32 * blk + NT * part:32 * blk + NT * part + NT, :]).then_inc(max_rows, 16)

            def ffn(ph):
                for b in range(B):
                    store_parts(ph * B + b, b)
                    sp.wait_ge(parts_stored, 96 * (B * ph + b + 1))
                    if b == 0:
                        sp.wait_ge(stacks_clear, 5 * ph + 4)
                        for g in range(NB):
                            load_stacks(g, ph * UNITS + g, g, ph == 0)
                max_rows_in(0, ph * UNITS)

                def body(ul, first, last):
                    for g in range(NB):
                        u = ph * UNITS + ul + g
                        if not (last and g == NB - 1):
                            max_rows_in((g + 1) % NB, u + 1)
                        if not (first and g == 0):
                            store_o((g - 1) % NB, u - 1, ul + g - 1)
                        if not last:
                            load_stacks(g, u + NB, ul + g + NB, False)
                body(0, True, False)
                with sp.Fori(1, UNITS // NB - 1) as i:
                    body(i * NB, False, False)
                body(UNITS - NB, False, True)
                store_o(NB - 1, (ph + 1) * UNITS - 1, UNITS - 1)
                for b in range(B):
                    if b == 0:
                        for par in range(2):
                            sp.wait_ge(o_stored[par], 32 * UNITS * (ph + 1))
                    sp.wait_ge(on_ready, ph * B + b)
                    for kind in range(2):
                        for g in range(4):
                            sp.dma_start(o_all[:, kind, g // 2, (g % 2) * HALF:(g % 2 + 1) * HALF],
                                         o_dram.ap()[b * FH:(b + 1) * FH, g, kind * FD:(kind + 1) * FD, :]).then_inc(o_loaded, 16)

            def load_wq(par, pg, pl):
                if not isinstance(pg, int) or pg >= 2:
                    sp.wait_ge(proj_done, 2 * pg - 2)
                sp.dma_start(wq_pair[:, par, :], a_wq[:, bass.ds(pl * 2 * AD, 2 * AD)]).then_inc(wq_loaded[par], 16)

            def build_q_s(par, pg):
                sp.wait_ge(q3_ready, 2 * pg + 2)
                if not isinstance(pg, int) or pg >= 2:
                    sp.wait_ge(a_scores, NS * pg - NS)
                for hh in range(2):
                    rows = slice(hh * AD, (hh + 1) * AD)
                    sp.dma_start(q_s[AD:P, par, hh, :, :], q_part[rows, :, :]).then_inc(q_s_loaded[par], 16)
                    sp.dma_start(q_s[0:AD, par, hh, 0:2, :], q_part[rows, 0:2, :]).then_inc(q_s_loaded[par], 16)
                    sp.dma_start(q_s[0:AD, par, hh, 2, :], q_part[rows, 0, :]).then_inc(q_s_loaded[par], 16)

            def attention():
                for k in range(2):
                    load_wq(k, k, k)
                build_q_s(0, 0)

                def body(b, pl, last):
                    for k in range(2):
                        pg = b * PAIRS + pl + k
                        if not (last and k == 1):
                            build_q_s((k + 1) % 2, pg + 1)
                        if not last:
                            nxt = pl + k + 2
                            load_wq(k, pg + 2, nxt % PAIRS if isinstance(nxt, int) else nxt)
                for b in range(B):
                    body(b, 0, False)
                    with sp.Fori(1, PAIRS // 2 - 1) as i:
                        body(b, i * 2, False)
                    body(b, PAIRS - 2, b == B - 1)

            ffn(0)
            attention()
            ffn(1)
            for b in range(B):
                sp.wait_ge(x_ready, 4 * B + 2 * b + 2)
                sp.dma_start(out[b].rearrange("(t p) c -> p t c", p=P), x[:, b * NT:(b + 1) * NT, :]).then_inc(out_stored, 16)
            sp.wait_ge(out_stored, 16 * B)

        @block.gpsimd
        def _(pool):
            nc.gpsimd.memset(ident[:, :], 1.0).then_inc(const_ready, 1)
            nc.gpsimd.memset(tri[:, :, :], 1.0).then_inc(const_ready, 1)
            pool.wait_ge(const_ready, 2)
            nc.gpsimd.affine_select(out=ident[:, :], in_=ident[:, :], compare_op=ALU.is_equal, fill=0.0, base=0,
                                    pattern=[[-1, P]], channel_multiplier=1).then_inc(const_ready, 1)
            nc.gpsimd.affine_select(out=tri[:, :, :], in_=tri[:, :, :], compare_op=ALU.is_ge, fill=0.0, base=-1,
                                    pattern=[[1, E], [-1, E]], channel_multiplier=0).then_inc(const_ready, 1)
            nc.gpsimd.memset(max_parts[:, :], 0.0).then_inc(const_ready, 1)
            pool.wait_ge(const_ready, 5)

            def wait(semaphore, value):
                pool.wait_ge(semaphore, value)
                pool.sem_inc(pool_waited, 1)

            nc.gpsimd.memset(causal[:, :], 0.0).then_inc(const_ready, 1)
            nc.gpsimd.tensor_copy(ident_bf[:, :], ident[:, :]).then_inc(const_ready, 1)
            nc.gpsimd.memset(null_sel[:, :], 0.0).then_inc(const_ready, 1)
            pool.wait_ge(const_ready, 8)
            nc.gpsimd.affine_select(out=causal[:, :], in_=causal[:, :], compare_op=ALU.is_ge, fill=MASKED, base=0,
                                    pattern=[[-1, P]], channel_multiplier=1).then_inc(const_ready, 1)
            pool.wait_ge(const_ready, 9)
            pool.wait_ge(aw_loaded, 16 * 5)
            for h in range(2):
                nc.gpsimd.tensor_copy(null_sel[h * AD:(h + 1) * AD, h:h + (PAIRS - 1) * (AH + 2) + 1:AH + 2],
                                      null_col[h * AD:(h + 1) * AD, :].broadcast_to([AD, PAIRS])).then_inc(const_ready, 1)
                pool.wait_ge(const_ready, 10 + h)

            def split(f):
                for c in range(4):
                    k, s = c // 2, slice((c % 2) * HALF, (c % 2 + 1) * HALF)
                    pool.wait_ge(part1_ready, 4 * f + c + 1)
                    nc.gpsimd.tensor_tensor(qkr[:, k, s], qkf[:, k, s], parts[:, k, 0, s], ALU.subtract).then_inc(rest_ready, 1)
                for c in range(4):
                    k, s = c // 2, slice((c % 2) * HALF, (c % 2 + 1) * HALF)
                    pool.wait_ge(part2_ready, 4 * f + c + 1)
                    nc.gpsimd.tensor_tensor(parts[:, k, 2, s], qkr[:, k, s], parts[:, k, 1, s], ALU.subtract).then_inc(part3_ready, 1)

            def prepare(g, u, ul, first):
                if not first:
                    wait(scores_done, TB * u - TB * (NB - 1))
                    wait(pv_done, NT // 2 * u - NT // 2 * (NB - 1))
                nc.gpsimd.memset(q_stack[96:98, g, :], 0.0).then_inc(rows_zeroed, 1)
                wait(rows_zeroed, u + 1)
                nc.gpsimd.tensor_copy(v_unit[:, g, :, 0:FD],
                                      v_all[:, bass.ds(ul, 1), :, :].rearrange("p u k d -> p (u k) d")).then_inc(v_unit_ready, 1)
                wait(v_unit_ready, u + 1)

            def clear_stacks(ph):
                if ph:
                    pool.wait_ge(x_ready, 4 * B)
                nc.gpsimd.memset(q_stack[:, :, :], 0.0).then_inc(stacks_clear, 1)
                nc.gpsimd.memset(k_stack[:, :, :], 0.0).then_inc(stacks_clear, 1)
                nc.gpsimd.memset(v_unit[:, :, :, :], 0.0).then_inc(stacks_clear, 1)
                pool.wait_ge(stacks_clear, 5 * ph + 3)
                nc.gpsimd.memset(k_stack[96:98, :, :], 1.0).then_inc(stacks_clear, 1)
                pool.wait_ge(stacks_clear, 5 * ph + 4)
                nc.gpsimd.memset(v_unit[:, :, :, FD:2 * FD], 1.0).then_inc(stacks_clear, 1)
                pool.wait_ge(stacks_clear, 5 * ph + 5)

            def ffn(ph):
                clear_stacks(ph)
                for b in range(B):
                    split(ph * B + b)
                pool.wait_ge(part3_ready, 4 * B * (ph + 1))
                pool.wait_ge(v_ready, 2 * B * (ph + 1))
                for g in range(NB - 1):
                    prepare(g, ph * UNITS + g, g, ph == 0)

                def body(ul, last):
                    for g in range(NB):
                        if not last or g == 0:
                            prepare((g - 1) % NB, ph * UNITS + ul + g - 1 + NB, ul + g - 1 + NB, False)
                body(0, False)
                with pool.Fori(1, UNITS // NB - 1) as i:
                    body(i * NB, False)
                body(UNITS - NB, True)

            def q_third(pg, h):
                s = slice(h * HALF, (h + 1) * HALF)
                wait(q2_ready, 2 * pg + h + 1)
                nc.gpsimd.tensor_tensor(q_part[:, 2, s], q_rest[:, s], q_part[:, 1, s], ALU.subtract).then_inc(q3_ready, 1)
                wait(q3_ready, 2 * pg + h + 1)

            def normalize(pg, t):
                n = 1 + (STEPS[t][2] + 1) * P
                wait(a_rsum_ready, NS * pg + t + 1)
                nc.gpsimd.tensor_scalar(a_probs[:, t % RING, 1:n], a_probs[:, t % RING, 1:n], a_rsum[:, t:t + 1], 1.0,
                                        ALU.mult, ALU.mult).then_inc(a_normed, 1)
                wait(a_normed, NS * pg + t + 1)

            def attention():
                for h in range(2):
                    q_third(0, h)

                def body(b, pl, switch, last):
                    for k in range(2):
                        pg = b * PAIRS + pl + k
                        q_steps = LATE_Q_STEPS if switch and k == 0 else Q_STEPS
                        for t in range(NS):
                            normalize(pg, t)
                            if t - 1 in q_steps and not (last and k == 1):
                                q_third(pg + 1, q_steps.index(t - 1))
                for b in range(B):
                    body(b, 0, b > 0, False)
                    with pool.Fori(1, PAIRS // 2 - 1) as i:
                        body(b, i * 2, False, False)
                    body(b, PAIRS - 2, False, b == B - 1)

            ffn(0)
            attention()
            ffn(1)

        @block.scalar
        def _(act):
            act.wait_ge(eps_ready, 1)
            act.sem_inc(probs_ready, TB)

            def norm_std(n, b):
                act.wait_ge(mv_ready, n + 1)
                nc.scalar.activation(rstd[:, b * NT:(b + 1) * NT], mean_var[:, b * NT:(b + 1) * NT, 1], ACT.Sqrt,
                                     bias=eps_col[:, 0:1]).then_inc(std_ready, 1)

            def norm_T(n, b, bank=0):
                for h in range(2):
                    act.wait_ge(xT_done, 2 * n + h + 1)
                    nc.scalar.activation(xnT[:, b, h * HALF:(h + 1) * HALF], ps[:, bank + h, :], ACT.Copy,
                                         accum_out=tok_sum[:, b, h:h + 1]).then_inc(xnT_ready, 1)

            def gates(f, b):
                act.wait_ge(hid_done, f + 1)
                nc.scalar.activation(hid[:, :], ps[:, 6, 0:1].to_broadcast([P, P]), ACT.Relu, bias=bg1[:, 0:1],
                                     scale=1.0 / T).then_inc(hid_ready, 1)
                act.wait_ge(gexp_in, f + 1)
                nc.scalar.activation(g_s[:, 1, :], g_s[:, 0, :], ACT.Exp).then_inc(gexp_out, 1)

            def split(f):
                for c in range(4):
                    k, s = c // 2, slice((c % 2) * HALF, (c % 2 + 1) * HALF)
                    act.wait_ge(qkf_ready, 4 * f + c + 1)
                    if f:
                        act.wait_ge(parts_stored, 96 * f)
                    nc.scalar.activation(parts[:, k, 0, s], qkf[:, k, s], ACT.Copy).then_inc(part1_ready, 1)
                for c in range(4):
                    k, s = c // 2, slice((c % 2) * HALF, (c % 2 + 1) * HALF)
                    act.wait_ge(rest_ready, 4 * f + c + 1)
                    nc.scalar.activation(parts[:, k, 1, s], qkr[:, k, s], ACT.Copy).then_inc(part2_ready, 1)

            def wait(semaphore, value):
                act.wait_ge(semaphore, value)
                act.sem_inc(act_waited, 1)

            def values_out(b):
                act.wait_ge(av_done, b + 1)
                nc.scalar.activation(av[:, b, :, :].rearrange("p t d -> p (t d)"), ps[:, 4, :], ACT.Copy).then_inc(av_ready, 1)

            def key_part(b, k):
                if k == 0:
                    act.wait_ge(kvf_ready, b + 1)
                    nc.scalar.activation(k_b[:, b, 0:KEYS], kvf[:, 0:KEYS], ACT.Copy).then_inc(k_split, 1)
                elif k == 1:
                    act.wait_ge(kvr_ready, b + 1)
                    nc.scalar.activation(k_a[:, b, 0:KEYS], kvr[:, 0:KEYS], ACT.Copy).then_inc(k_split, 1)
                else:
                    act.wait_ge(k3_ready, b + 1)
                    nc.scalar.activation(k_a[0:AD, b, 0:KEYS], kvf[0:AD, 0:KEYS], ACT.Copy).then_inc(keys_ready, 1)

            def q_first(pg, par, h):
                if h == 0 and (not isinstance(pg, int) or pg >= 1):
                    act.wait_ge(q_s_loaded[1 - par], 48 * (pg - 1 - (1 - par)) + 96)
                act.wait_ge(proj_done, 2 * pg + h + 1)
                nc.scalar.activation(q_part[:, 0, h * HALF:(h + 1) * HALF], ps[:, PV_BANK, :], ACT.Copy,
                                     scale=A_SCALE).then_inc(q1_ready, 1)

            def q_second(pg, h, k):
                act.wait_ge(pv_bank_free, k + 1)
                nc.scalar.activation(q_part[:, 1, h * HALF:(h + 1) * HALF], q_rest[:, h * HALF:(h + 1) * HALF],
                                     ACT.Copy).then_inc(q2_ready, 1)

            def a_exps(pg, t):
                qh, hh, qt = STEPS[t]
                n = 1 + (qt + 1) * P
                act.wait_ge(a_max, NS * pg + t + 1)
                if t >= RING or not isinstance(pg, int) or pg >= 1:
                    before, pair = (t - RING, pg) if t >= RING else (NS + t - RING, pg - 1)
                    use = FIRST_USE[before] + len(USES[before]) - 1
                    act.wait_ge(tr_done[use % 2], N_USES // 2 * pair + use // 2 + 1)
                nc.scalar.activation(a_probs[:, t % RING, 0:n],
                                     ps[:, S_BANK[t % 2]:S_BANK[t % 2] + (n + HALF - 1) // HALF, :].rearrange("p a b -> p (a b)")[:, 0:n],
                                     ACT.Exp, bias=a_neg_max[:, t:t + 1], accum_out=a_sum[:, t:t + 1]).then_inc(a_exp, 1)

            def a_evac(pg, t):
                qh, hh, qt = STEPS[t]
                for k, (kt, m) in enumerate(USES[t]):
                    use = FIRST_USE[t] + k
                    if use % 2 == 1:
                        act.wait_ge(tr_done[1], N_USES // 2 * pg + use // 2 + 1)
                        nc.scalar.activation(probs_T[qh][:, hh, kt:kt + m, (qt % 4) * P:(qt % 4 + 1) * P],
                                             ps[:, T_BANK[1], 0:m * P].rearrange("p (k q) -> p k q", q=P), ACT.Copy).then_inc(evac_act, 1)

            def p0_evac(b, h, bank):
                act.wait_ge(p0T_done, 2 * b + h + 1)
                if b and h == 0:
                    act.wait_ge(ay_done, 2 * b)
                nc.scalar.activation(p0_T[:, h * HALF:(h + 1) * HALF], ps[0:AH, bank, :], ACT.Copy).then_inc(p0T_ready, 1)

            def attention():
                norm_std(B, 0)
                norm_T(B, 0, 5)
                act.wait_ge(x_ready, 2 * B)
                q_first(0, 0, 0)
                values_out(0)
                key_part(0, 0)
                q_second(0, 0, 0)
                q_first(0, 0, 1)
                key_part(0, 1)
                q_second(0, 1, 1)
                key_part(0, 2)
                for b in range(1, B):
                    norm_std(B + b, b)
                    norm_T(B + b, b, 5)
                    values_out(b)
                    for k in range(3):
                        key_part(b, k)
                act.wait_ge(null_done, 1)
                nc.scalar.activation(null_out[:, :], ps[0:AH, 5, 0:C], ACT.Copy).then_inc(null_ready, 1)

                def body(b, pl, switch, first, last):
                    for k in range(2):
                        pg = b * PAIRS + pl + k
                        turn = switch and k == 0
                        q_steps = LATE_Q_STEPS if turn else Q_STEPS
                        for t in range(NS):
                            if t > A_LAG:
                                a_evac(pg, t - A_LAG - 1)
                            elif not (first and k == 0):
                                a_evac(pg - 1, NS + t - A_LAG - 1)
                            if turn and t - 1 in P0_STEPS:
                                p0_evac(b - 1, P0_STEPS.index(t - 1), PV_BANK)
                            a_exps(pg, t)
                            if t in q_steps and not (last and k == 1):
                                q_first(pg + 1, (k + 1) % 2, q_steps.index(t))
                            if t - 1 in q_steps and not (last and k == 1):
                                h = q_steps.index(t - 1)
                                q_second(pg + 1, h, 4 * pg + 2 + h)
                for b in range(B):
                    body(b, 0, b > 0, b == 0, False)
                    with act.Fori(1, PAIRS // 2 - 1) as i:
                        body(b, i * 2, False, False, False)
                    body(b, PAIRS - 2, False, False, b == B - 1)
                for t in range(NS - A_LAG - 1, NS):
                    a_evac(B * PAIRS - 1, t)
                for h in range(2):
                    p0_evac(B - 1, h, 2 + h)

            def evacuate(g, u):
                act.wait_ge(pv_done, NT // 2 * u + NT // 2)
                act.wait_ge(o_stored[g % 2], 32 * (u - g % 2))
                nc.scalar.activation(o_unit[:, g % 2, :], ps[:, PV_BANK, :], ACT.Copy).then_inc(o_ready, 1)

            def exps(g, u, first):
                for t in range(TB):
                    act.wait_ge(scores_done, TB * u + t + 1)
                    if t % 4 == 0 and not first:
                        act.wait_ge(pv_done, NT // 2 * u - NT // 2 + t // 4 + 1)
                    nc.scalar.activation(probs[:, t, :], ps[:, EXP_BANK[t], :], ACT.Exp, scale=F_SCALE).then_inc(probs_ready, 1)
                    if t == 4 and not first:
                        evacuate((g - 1) % NB, u - 1)

            def ffn(ph):
                for b in range(B):
                    norm_std(2 * ph * B + b, b)
                    norm_T(2 * ph * B + b, b)
                    gates(ph * B + b, b)
                    split(ph * B + b)

                def body(ul, first):
                    for g in range(NB):
                        exps(g, ph * UNITS + ul + g, first and g == 0)
                body(0, True)
                with act.Fori(1, UNITS // NB) as i:
                    body(i * NB, False)
                evacuate(NB - 1, ph * UNITS + UNITS - 1)

            ffn(0)
            attention()
            ffn(1)

        @block.vector
        def _(dve):
            made = [0]

            def link(ins):
                made[0] += 1
                ins.then_inc(dve_link, 1)
                dve.wait_ge(dve_link, made[0])

            nc.vector.memset(eps_col[:, :], EPS).then_inc(eps_ready, 1)
            dve.sem_inc(max_read, 2)

            def norm(n, b):
                if n < B:
                    dve.wait_ge(x_loaded[b], 16)
                else:
                    dve.wait_ge(x_ready, 2 * (n - B) + 2)
                for t in range(b * NT, (b + 1) * NT):
                    ins = nc.vector.bn_stats(stats[:, t, :], x[:, t, :])
                link(ins)
                for t in range(b * NT, (b + 1) * NT):
                    ins = nc.vector.bn_aggr(mean_var[:, t, :], stats[:, t, :])
                ins.then_inc(mv_ready, 1)
                dve.wait_ge(std_ready, n + 1)
                if n:
                    dve.wait_ge(xT_done, 2 * n)
                link(nc.vector.reciprocal(rstd[:, b * NT:(b + 1) * NT], rstd[:, b * NT:(b + 1) * NT]))
                for t in range(b * NT, (b + 1) * NT):
                    ins = nc.vector.tensor_scalar(xn[:, t % NT, :], x[:, t, :], mean_var[:, t, 0:1], rstd[:, t:t + 1],
                                                  ALU.subtract, ALU.mult)
                    if t % 4 == 3:
                        ins.then_inc(xn_ready, 1)

            def gating(f, b):
                dve.wait_ge(logits_done, f + 1)
                if f == 0:
                    dve.wait_ge(w_loaded, 16 * 12)
                    dve.wait_ge(const_ready, 5)
                link(nc.vector.tensor_tensor(lg[:, :], ps[:, 6, 8:8 + E], bg2[:, :], ALU.add))
                other = lg[:, :].unsqueeze(1).broadcast_to([P, E, E])
                own = lg[:, :].unsqueeze(2).broadcast_to([P, E, E])
                nc.vector.tensor_tensor(g_cmp[:, :, :], other, own, ALU.is_gt)
                link(nc.vector.tensor_tensor(g_eq[:, :, :], other, own, ALU.is_equal))
                link(nc.vector.tensor_tensor(g_eq[:, :, :], g_eq[:, :, :], tri[:, :, :], ALU.mult))
                link(nc.vector.tensor_tensor(g_cmp[:, :, :], g_cmp[:, :, :], g_eq[:, :, :], ALU.add))
                nc.vector.reduce_sum(g_s[:, 2, :], g_cmp[:, :, :], AX)
                link(nc.vector.reduce_max(g_s[:, 3, 0:1], lg[:, :], AX))
                link(nc.vector.tensor_scalar(g_s[:, 4, :], g_s[:, 2, :], 1.5, None, ALU.is_lt))
                nc.vector.tensor_scalar(g_s[:, 0, :], lg[:, :], g_s[:, 3, 0:1], None, ALU.subtract).then_inc(gexp_in, 1)
                dve.wait_ge(gexp_out, f + 1)
                link(nc.vector.tensor_tensor(g_s[:, 5, :], g_s[:, 1, :], g_s[:, 4, :], ALU.mult))
                link(nc.vector.reduce_sum(g_s[:, 6, 0:1], g_s[:, 5, :], AX))
                link(nc.vector.reciprocal(g_s[:, 7, 0:1], g_s[:, 6, 0:1]))
                link(nc.vector.tensor_scalar(gate[:, b, :], g_s[:, 5, :], g_s[:, 7, 0:1], None, ALU.mult))
                wm = w_mix[:, b].rearrange("p k d -> p (k d)")
                bm = b_mix[:, b, :]
                for e in range(E):
                    we = w_experts[:, e].rearrange("p k d -> p (k d)")
                    be = b_experts[:, :, e]
                    ge = gate[:, b, e:e + 1]
                    if e == 0:
                        nc.vector.tensor_scalar(bm, be, ge, None, ALU.mult)
                        link(nc.vector.tensor_scalar(wm, we, ge, None, ALU.mult))
                    else:
                        nc.vector.scalar_tensor_tensor(bm, be, ge, bm, ALU.mult, ALU.add)
                        ins = nc.vector.scalar_tensor_tensor(wm, we, ge, wm, ALU.mult, ALU.add)
                        if e < E - 1:
                            link(ins)
                        else:
                            ins.then_inc(mix_ready, 1)

            def project(f, b):
                dve.wait_ge(mix_ready, f + 1)
                for c in range(4):
                    k, s = c // 2, slice((c % 2) * HALF, (c % 2 + 1) * HALF)
                    dve.wait_ge(qk_done, 4 * f + c + 1)
                    if f:
                        dve.wait_ge(rest_ready, 4 * f)
                        dve.wait_ge(part1_ready, 4 * f)
                    nc.vector.tensor_scalar(qkf[:, k, s], ps[:, 2 + c, :], b_mix[:, b, k:k + 1], None, ALU.add).then_inc(qkf_ready, 1)
                for g in range(2):
                    dve.wait_ge(vproj_done, 2 * f + g + 1)
                    for t in range(4):
                        ins = nc.vector.tensor_tensor(
                            v_all[:, b * FH:(b + 1) * FH, 4 * g + t, :],
                            ps[:, 6 + g, t * C:(t + 1) * C].rearrange("p (h d) -> p h d", d=FD),
                            w_mix[:, b, 3, :].rearrange("p (h d) -> p h d", d=FD), ALU.add)
                    ins.then_inc(v_ready, 1)

            def maxima(g, u):
                for t in range(NT):
                    dve.wait_ge(max_scores, NT * u + t + 1)
                    bank = MAX_BANK[t % 2]
                    nc.vector.tensor_reduce(neg_max[:, g, t:t + 1], ps[:, bank:bank + 2, :].rearrange("p a b -> p (a b)"), AX,
                                            ALU.max, negate=True).then_inc(max_read, 1)
                dve.wait_ge(max_read, 2 + NT * u + NT)
                nc.vector.tensor_copy(max_parts[:, 0:NT], neg_max[:, g, :]).then_inc(max_link, 1)
                dve.wait_ge(max_link, 2 * u + 1)
                nc.vector.tensor_tensor(max_parts[:, NT:2 * NT], neg_max[:, g, :], max_parts[:, 0:NT], ALU.subtract).then_inc(max_link, 1)
                dve.wait_ge(max_link, 2 * u + 2)
                dve.wait_ge(max_rows, 128 * u + 16)
                nc.vector.transpose(max_T[:, :], max_parts[:, :]).then_inc(max_T_ready, 1)

            def finish(f, b):
                dve.wait_ge(o_loaded, 128 * (f + 1))
                nc.vector.tensor_tensor(num[:, :], o_all[:, 0, 0, :], o_all[:, 0, 1, :], ALU.add)
                link(nc.vector.tensor_tensor(den[:, :], o_all[:, 1, 0, :], o_all[:, 1, 1, :], ALU.add))
                link(nc.vector.reciprocal(den[:, :], den[:, :]))
                nc.vector.tensor_tensor(num[:, :], num[:, :], den[:, :], ALU.mult).then_inc(on_ready, 1)
                for g in range(2):
                    xs = x[:, b * NT + 4 * g:b * NT + 4 * g + 4, :]
                    dve.wait_ge(y_done, 2 * f + g + 1)
                    n = f if f < B else f + B
                    dve.wait_ge(x_ready, 2 * n + g)
                    nc.vector.tensor_tensor(ytmp[:, :, :], ps[:, g, :].rearrange("p (t c) -> p t c", c=C),
                                            bo[:, :].unsqueeze(1).broadcast_to([P, 4, C]), ALU.add).then_inc(dve_link, 1)
                    made[0] += 1
                    dve.wait_ge(dve_link, made[0])
                    nc.vector.scalar_tensor_tensor(xs, ytmp[:, :, :], 0.5, xs, ALU.mult, ALU.add).then_inc(x_ready, 1)

            def keys_in(b):
                if b:
                    dve.wait_ge(keys_ready, b)
                for h in range(2):
                    dve.wait_ge(kv_done, 2 * b + h + 1)
                    ins = nc.vector.tensor_copy(kvf[:, 1 + h * HALF:1 + (h + 1) * HALF], ps[:, 2 + h, :])
                nc.vector.tensor_copy(kvf[:, 0:1], null_col[:, :]).then_inc(kvf_ready, 1)

            def keys_rest(b):
                dve.wait_ge(k_split, 2 * b + 1)
                nc.vector.tensor_tensor(kvr[:, 0:KEYS], kvf[:, 0:KEYS], k_b[:, b, 0:KEYS], ALU.subtract).then_inc(kvr_ready, 1)
                dve.wait_ge(k_split, 2 * b + 2)
                nc.vector.tensor_tensor(k_b[0:AD, b, 0:KEYS], kvr[0:AD, 0:KEYS], k_a[0:AD, b, 0:KEYS], ALU.subtract).then_inc(k3_ready, 1)

            def q_rests(pg, h):
                if h == 0 and (not isinstance(pg, int) or pg >= 1):
                    dve.wait_ge(q3_ready, 2 * pg)
                dve.wait_ge(q1_ready, 2 * pg + h + 1)
                s = slice(h * HALF, (h + 1) * HALF)
                nc.vector.scalar_tensor_tensor(q_rest[:, s], ps[:, PV_BANK, :], A_SCALE, q_part[:, 0, s], ALU.mult,
                                               ALU.subtract).then_inc(pv_bank_free, 1)

            def a_maximum(pg, t):
                n = 1 + (STEPS[t][2] + 1) * P
                dve.wait_ge(a_scores, NS * pg + t + 1)
                nc.vector.tensor_reduce(a_neg_max[:, t:t + 1],
                                        ps[:, S_BANK[t % 2]:S_BANK[t % 2] + (n + HALF - 1) // HALF, :].rearrange("p a b -> p (a b)")[:, 0:n],
                                        AX, ALU.max, negate=True).then_inc(a_max, 1)

            def a_recip(pg, b, pl, t):
                qh, hh, qt = STEPS[t]
                dve.wait_ge(a_exp, NS * pg + t + 1)
                nc.vector.reciprocal(a_rsum[:, t:t + 1], a_sum[:, t:t + 1]).then_inc(a_rsum_ready, 1)
                dve.wait_ge(a_rsum_ready, NS * pg + t + 1)
                nc.vector.tensor_tensor(p0[:, b, qt, bass.ds(2 * pl + hh, 1)], a_probs[:, t % RING, 0:1], a_rsum[:, t:t + 1],
                                        ALU.mult).then_inc(p0_ready, 1)

            def a_evac(pg, t):
                qh, hh, qt = STEPS[t]
                for k, (kt, m) in enumerate(USES[t]):
                    use = FIRST_USE[t] + k
                    if use % 2 == 0:
                        dve.wait_ge(tr_done[0], N_USES // 2 * pg + use // 2 + 1)
                        nc.vector.tensor_copy(probs_T[qh][:, hh, kt:kt + m, (qt % 4) * P:(qt % 4 + 1) * P],
                                              ps[:, T_BANK[0], 0:m * P].rearrange("p (k q) -> p k q", q=P)).then_inc(evac_dve, 1)

            def o_evac(pg, pl, qh):
                dve.wait_ge(apv_done, 2 * pg + qh + 1)
                nc.vector.tensor_scalar(o_T[:, bass.ds(pl, 1), qh * HALF:(qh + 1) * HALF].rearrange("p a b -> p (a b)"),
                                        ps[:, PV_BANK, :], 1.0, None, ALU.mult).then_inc(pv_bank_free, 1)

            def add_out(b, g, bank):
                dve.wait_ge(ay_done, 2 * b + g + 1)
                xs = x[:, b * NT + 4 * g:b * NT + 4 * g + 4, :].rearrange("p t c -> p (t c)")
                nc.vector.tensor_tensor(xs, ps[:, bank, :], xs, ALU.add).then_inc(x_ready, 1)

            def attention():
                q_rests(0, 0)
                keys_in(0)
                q_rests(0, 1)
                keys_rest(0)
                for b in range(1, B):
                    norm(B + b, b)
                    keys_in(b)
                    keys_rest(b)

                def body(b, pl, switch, first, last):
                    for k in range(2):
                        pg = b * PAIRS + pl + k
                        turn = switch and k == 0
                        q_steps = LATE_Q_STEPS if turn else Q_STEPS
                        before = (b - 1, PAIRS - 1) if turn else (b, pl + k - 1)
                        for t in range(NS):
                            if t > A_LAG:
                                a_evac(pg, t - A_LAG - 1)
                            elif not (first and k == 0):
                                a_evac(pg - 1, NS + t - A_LAG - 1)
                            if t >= 2:
                                a_recip(pg, b, pl + k, t - 2)
                            elif not (first and k == 0):
                                a_recip(pg - 1, *before, NS + t - 2)
                            a_maximum(pg, t)
                            if t == A_LAG + 1 and not (first and k == 0):
                                o_evac(pg - 1, before[1], 1)
                            if turn and t - 1 in Y_STEPS:
                                add_out(b - 1, Y_STEPS.index(t - 1), PV_BANK)
                            if t in q_steps and not (last and k == 1):
                                q_rests(pg + 1, q_steps.index(t))
                            if t == 9 + A_LAG:
                                if first and k == 0:
                                    dve.wait_ge(keys_ready, B)
                                o_evac(pg, pl + k, 0)
                for b in range(B):
                    body(b, 0, b > 0, b == 0, False)
                    with dve.Fori(1, PAIRS // 2 - 1) as i:
                        body(b, i * 2, False, False, False)
                    body(b, PAIRS - 2, False, False, b == B - 1)
                pg = B * PAIRS - 1
                for t in range(NS - 2, NS):
                    a_recip(pg, B - 1, PAIRS - 1, t)
                for t in range(NS - A_LAG - 1, NS):
                    a_evac(pg, t)
                o_evac(pg, PAIRS - 1, 1)
                for g in range(2):
                    add_out(B - 1, g, g)

            def ffn(ph):
                for b in range(B):
                    norm(2 * ph * B + b, b)
                    gating(ph * B + b, b)
                    project(ph * B + b, b)
                with dve.Fori(0, UNITS // NB) as i:
                    for g in range(NB):
                        maxima(g, ph * UNITS + i * NB + g)
                for b in range(B):
                    finish(ph * B + b, b)
                    if ph == 0 and b == 0:
                        norm(B, 0)

            ffn(0)
            attention()
            ffn(1)

        @block.tensor
        def _(pe):
            pe.wait_ge(const_ready, 5)
            pe.wait_ge(w_loaded, 16 * 12)

            def norm_T(n, b, bank=0):
                for h in range(2):
                    pe.wait_ge(xn_ready, 2 * n + h + 1)
                    for t in range(4):
                        ins = nc.tensor.transpose(ps[:, bank + h, t * P:(t + 1) * P], xn[:, 4 * h + t, :], ident[:, :])
                    ins.then_inc(xT_done, 1)

            def gates(n, f, b):
                pe.wait_ge(xnT_ready, 2 * n + 2)
                for h in range(2):
                    ins = nc.tensor.matmul(ps[:, 6, 0:1], wg1[:, :], tok_sum[:, b, h:h + 1], start=h == 0, stop=h == 1)
                ins.then_inc(hid_done, 1)
                pe.wait_ge(hid_ready, f + 1)
                nc.tensor.matmul(ps[:, 6, 8:8 + E], hid[:, :], wg2[:, :], start=True, stop=True).then_inc(logits_done, 1)

            def project(f, b):
                pe.wait_ge(mix_ready, f + 1)
                if f:
                    pe.wait_ge(qkf_ready, 4 * f)
                    pe.wait_ge(v_ready, 2 * f)
                for c in range(4):
                    nc.tensor.matmul(ps[:, 2 + c, :], w_mix[:, b, c // 2, :], xnT[:, b, (c % 2) * HALF:(c % 2 + 1) * HALF],
                                     start=True, stop=True).then_inc(qk_done, 1)
                for g in range(2):
                    for t in range(4):
                        ins = nc.tensor.matmul(ps[:, 6 + g, t * C:(t + 1) * C], xnT[:, b, (4 * g + t) * P:(4 * g + t + 1) * P],
                                               w_mix[:, b, 2, :], start=True, stop=True)
                    ins.then_inc(vproj_done, 1)

            def max_tile(g, u, t):
                if t == 0:
                    pe.wait_ge(stacks_loaded[g], 64 // NB * (u - g) + 64)
                    pe.wait_ge(rows_zeroed, u + 1)
                pe.wait_ge(max_read, NT * u + t + 1)
                bank = MAX_BANK[t % 2]
                for h in range(2):
                    ins = nc.tensor.matmul(ps[:, bank + h, :], q_stack[:, g, t * P:(t + 1) * P],
                                           k_stack[:, g, h * HALF:(h + 1) * HALF], start=True, stop=True)
                ins.then_inc(max_scores, 1)

            def score_tile(g, u, kt, h):
                if kt == 0 and h == 0:
                    pe.wait_ge(max_rows, 128 * u + 128 + 16)
                t = 2 * kt + h
                bank = EXP_BANK[t]
                before = max([s for s in range(t) if EXP_BANK[s] == bank] + [max(s for s in range(TB) if EXP_BANK[s] == bank) - TB
                                                                             if t < 3 else -TB])
                pe.wait_ge(probs_ready, TB + TB * u + before + 1)
                ins = nc.tensor.matmul(ps[:, bank, :], k_stack[:, g, kt * P:(kt + 1) * P],
                                       q_stack[:, g, h * HALF:(h + 1) * HALF], start=True, stop=True)
                ins.then_inc(scores_done, 1)

            def values(g, u, j):
                if j == 0:
                    pe.wait_ge(v_unit_ready, u + 1)
                    pe.wait_ge(o_ready, u)
                pe.wait_ge(probs_ready, TB + TB * u + 4 * j + 4)
                for t in range(4 * j, 4 * j + 4):
                    col = 32 * (t % 4)
                    ins = nc.tensor.matmul(ps[col:col + 32, PV_BANK, :], v_unit[:, g, t // 2, :], probs[:, t, :],
                                           start=j == 0, stop=j == NT // 2 - 1)
                ins.then_inc(pv_done, 1)

            LAG = 2

            def unit(g, u, first, ahead):
                for kt in range(NT):
                    score_tile(g, u, kt, 0)
                    if kt < NT - SHIFT and ahead > 0:
                        max_tile((g + 1) % NB, u + 1, SHIFT + kt)
                    elif kt >= NT - SHIFT and ahead > 1:
                        max_tile((g + 2) % NB, u + 2, kt - (NT - SHIFT))
                    score_tile(g, u, kt, 1)
                    if kt % 2 == 1:
                        j = kt // 2 - 1
                        if j >= 0:
                            values(g, u, j)
                        elif not first:
                            values((g - 1) % NB, u - 1, NT // 2 - 1)

            def finish(f, b):
                pe.wait_ge(on_ready, f + 1)
                for g in range(2):
                    for t in range(4):
                        ins = nc.tensor.matmul(ps[:, g, t * C:(t + 1) * C], num[:, (4 * g + t) * P:(4 * g + t + 1) * P],
                                               wo[:, :], start=True, stop=True)
                    ins.then_inc(y_done, 1)

            def keys(b):
                pe.wait_ge(xnT_ready, 2 * (2 + b) + 2)
                if b:
                    pe.wait_ge(kvf_ready, b)
                    pe.wait_ge(av_ready, b)
                for h in range(2):
                    nc.tensor.matmul(ps[:, 2 + h, :], wkv2[:, :, :].rearrange("p a b -> p (a b)"), xnT[:, b, h * HALF:(h + 1) * HALF],
                                     start=True, stop=True).then_inc(kv_done, 1)
                for t in range(NT):
                    ins = nc.tensor.matmul(ps[:, 4, t * AD:(t + 1) * AD], xnT[:, b, t * P:(t + 1) * P], wkv2[:, 0, :],
                                           start=True, stop=True)
                ins.then_inc(av_done, 1)

            def queries(pg, k, b, par, h):
                if h == 0:
                    pe.wait_ge(wq_loaded[par], 8 * (pg - par) + 16)
                if not isinstance(pg, int) or k > 0:
                    pe.wait_ge(pv_bank_free, k)
                nc.tensor.matmul(ps[:, PV_BANK, :], wq_pair[:, par, :], xnT[:, b, h * HALF:(h + 1) * HALF],
                                 start=True, stop=True).then_inc(proj_done, 1)

            def a_score_tile(pg, b, par, t):
                qh, hh, qt = STEPS[t]
                n = 1 + (qt + 1) * P
                if t == 0:
                    pe.wait_ge(q_s_loaded[par], 48 * (pg - par) + 96)
                if t >= 2 or not isinstance(pg, int) or pg >= 1:
                    pe.wait_ge(a_exp, NS * pg + t - 1)
                cols = slice(qt * P, (qt + 1) * P)
                for c0 in range(0, n, HALF):
                    c1 = min(n, c0 + HALF)
                    m0, m1 = max(c0, 1 + qt * P), c1
                    bank = S_BANK[t % 2] + c0 // HALF
                    passes = [(q_s[:, par, hh, k, cols], key[:, b, c0:c1], 0, c1 - c0) for k, key in enumerate((k_a, k_a, k_b))]
                    if m1 > m0:
                        passes.append((ident_bf[:, :], causal[:, m0 - 1 - qt * P:m1 - 1 - qt * P], m0 - c0, m1 - c0))
                    for k, (lhs, rhs, o0, o1) in enumerate(passes):
                        ins = nc.tensor.matmul(ps[:, bank, o0:o1], lhs, rhs, start=k == 0, stop=k == len(passes) - 1)
                ins.then_inc(a_scores, 1)

            def a_transposes(pg, t):
                qh, hh, qt = STEPS[t]
                pe.wait_ge(a_normed, NS * pg + t + 1)
                for k, (kt, m) in enumerate(USES[t]):
                    use = FIRST_USE[t] + k
                    if use >= 2 or not isinstance(pg, int) or pg >= 1:
                        pe.wait_ge(evac_act if use % 2 else evac_dve, N_USES // 2 * pg + use // 2)
                    for j in range(m):
                        ins = nc.tensor.transpose(ps[:, T_BANK[use % 2], j * P:(j + 1) * P],
                                                  a_probs[:, t % RING, 1 + (kt + j) * P:1 + (kt + j + 1) * P], ident[:, :])
                    ins.then_inc(tr_done[use % 2], 1)

            def a_values(pg, b, qh, k0):
                last = [s for s in range(NS) if STEPS[s][0] == qh][-1]
                done = (FIRST_USE[last] + len(USES[last])) // 2
                pe.wait_ge(evac_dve, N_USES // 2 * pg + done)
                pe.wait_ge(evac_act, N_USES // 2 * pg + done)
                pe.wait_ge(pv_bank_free, k0)
                nk = 4 * (qh + 1)
                for kt in range(nk):
                    q0 = max(0, kt - 4 * qh) * P
                    for hh in range(2):
                        ins = nc.tensor.matmul(ps[hh * AD:(hh + 1) * AD, PV_BANK, q0:HALF], av[:, b, kt, :],
                                               probs_T[qh][:, hh, kt, q0:HALF], start=kt == 0, stop=kt == nk - 1)
                ins.then_inc(apv_done, 1)

            def p0_transposes(b, h, bank):
                if h == 0:
                    pe.wait_ge(p0_ready, NS * PAIRS * (b + 1))
                for t in range(4):
                    ins = nc.tensor.transpose(ps[0:AH, bank, t * P:(t + 1) * P], p0[:, b, 4 * h + t, :], ident[:, :])
                ins.then_inc(p0T_done, 1)

            def outputs(b, g, bank):
                for t in range(4):
                    tok = slice((4 * g + t) * P, (4 * g + t + 1) * P)
                    for p in range(PAIRS):
                        nc.tensor.matmul(ps[:, bank, t * C:(t + 1) * C], o_T[:, p, tok], wout[:, p, :], start=p == 0, stop=False)
                    ins = nc.tensor.matmul(ps[:, bank, t * C:(t + 1) * C], p0_T[:, tok], null_out[:, :], start=False, stop=True)
                ins.then_inc(ay_done, 1)

            def attention():
                norm_T(B, 0, 5)
                pe.wait_ge(xnT_ready, 2 * B + 2)
                queries(0, 0, 0, 0, 0)
                keys(0)
                queries(0, 1, 0, 0, 1)
                for b in range(1, B):
                    norm_T(B + b, b, 5)
                    keys(b)
                pe.wait_ge(const_ready, 11)
                pe.wait_ge(xnT_ready, 2 * 2 * B)
                for p in range(PAIRS):
                    ins = nc.tensor.matmul(ps[0:AH, 5, 0:C], null_sel[:, p * AH:(p + 1) * AH], wout[:, p, :],
                                           start=p == 0, stop=p == PAIRS - 1)
                ins.then_inc(null_done, 1)
                pe.wait_ge(keys_ready, B)
                pe.wait_ge(av_ready, B)
                pe.wait_ge(null_ready, 1)

                def body(b, pl, switch, first, last):
                    for k in range(2):
                        pg = b * PAIRS + pl + k
                        turn = switch and k == 0
                        q_steps = LATE_Q_STEPS if turn else Q_STEPS
                        bb = b - 1 if turn else b
                        bn = b + 1 if isinstance(pl, int) and pl + k == PAIRS - 1 else b
                        for t in range(NS):
                            a_score_tile(pg, b, k, t)
                            if t >= A_LAG:
                                a_transposes(pg, t - A_LAG)
                            elif not (first and k == 0):
                                a_transposes(pg - 1, NS + t - A_LAG)
                            if t == A_LAG and not (first and k == 0):
                                a_values(pg - 1, bb, 1, 4 * (pg - 1) + 5)
                            if turn and t in P0_STEPS:
                                h = P0_STEPS.index(t)
                                if h == 0:
                                    pe.wait_ge(pv_bank_free, 4 * pg + 2)
                                else:
                                    pe.wait_ge(p0T_ready, 2 * (b - 1) + 1)
                                p0_transposes(b - 1, h, PV_BANK)
                            if turn and t in Y_STEPS:
                                g = Y_STEPS.index(t)
                                if g == 0:
                                    pe.wait_ge(p0T_ready, 2 * b)
                                else:
                                    pe.wait_ge(x_ready, 2 * B + 2 * b - 1)
                                outputs(b - 1, g, PV_BANK)
                            if t in q_steps and not (last and k == 1):
                                h = q_steps.index(t)
                                if turn and h == 0:
                                    pe.wait_ge(x_ready, 2 * B + 2 * b)
                                queries(pg + 1, 4 * pg + 2 + h, bn, (k + 1) % 2, h)
                            if t == 8 + A_LAG:
                                a_values(pg, b, 0, 4 * pg + (2 if last and k == 1 else 4))
                for b in range(B):
                    body(b, 0, b > 0, b == 0, False)
                    with pe.Fori(1, PAIRS // 2 - 1) as i:
                        body(b, i * 2, False, False, False)
                    body(b, PAIRS - 2, False, False, b == B - 1)
                pg = B * PAIRS - 1
                for t in range(NS - A_LAG, NS):
                    a_transposes(pg, t)
                a_values(pg, B - 1, 1, 4 * pg + 3)
                pe.wait_ge(a_exp, NS * (pg + 1))
                for h in range(2):
                    p0_transposes(B - 1, h, 2 + h)
                pe.wait_ge(p0T_ready, 2 * B)
                pe.wait_ge(pv_bank_free, 4 * (pg + 1))
                for g in range(2):
                    outputs(B - 1, g, g)

            def ffn(ph):
                for b in range(B):
                    norm_T(2 * ph * B + b, b)
                    gates(2 * ph * B + b, ph * B + b, b)
                    project(ph * B + b, b)
                pe.wait_ge(qkf_ready, 4 * B * (ph + 1))
                pe.wait_ge(v_ready, 2 * B * (ph + 1))
                u0 = ph * UNITS
                for t in range(NT):
                    max_tile(0, u0, t)
                for t in range(SHIFT):
                    max_tile(1, u0 + 1, t)
                for g in range(NB):
                    unit(g, u0 + g, g == 0, NB)
                with pe.Fori(1, UNITS // NB - 1) as i:
                    for g in range(NB):
                        unit(g, i * NB + (u0 + g), False, NB)
                for g in range(NB):
                    unit(g, u0 + UNITS - NB + g, False, NB - 1 - g)
                values(NB - 1, u0 + UNITS - 1, NT // 2 - 1)
                for b in range(B):
                    finish(ph * B + b, b)

            ffn(0)
            attention()
            ffn(1)


_INS = ["L0_attn_x", "L0_attn_Wq", "L0_attn_Wkv", "L0_attn_null_kv", "L0_attn_Wout", "L0_ffn_Wq", "L0_ffn_bq", "L0_ffn_Wk",
        "L0_ffn_bk", "L0_ffn_Wv", "L0_ffn_bv", "L0_ffn_Wg1", "L0_ffn_bg1", "L0_ffn_Wg2", "L0_ffn_bg2", "L0_ffn_Wo", "L0_ffn_bo"]


def kernel(**inputs):
    import numpy as _np
    import concourse.bacc as _bacc
    from concourse import mybir as _mybir
    from concourse.bass_utils import run_bass_kernel_spmd as _run

    nc = _bacc.Bacc("TRN2", target_bir_lowering=False, num_devices=1)
    arrays, args = {}, []
    for name in _INS:
        a = _np.ascontiguousarray(inputs[name])
        arrays[f"in_{name}"] = a
        args.append(nc.dram_tensor(f"in_{name}", a.shape, _mybir.dt.from_np(a.dtype), kind="ExternalInput").ap())
    x_shape = inputs["L0_attn_x"].shape
    args.append(nc.dram_tensor("out_0", x_shape, _mybir.dt.float32, kind="ExternalOutput").ap())
    build(nc, *args)
    r = _run(nc, [arrays], core_ids=[0])
    return r.results[0]["out_0"]
```

```python
from contextlib import ExitStack

import concourse.bass as bass
from concourse import mybir

F32 = mybir.dt.float32
BF16 = mybir.dt.bfloat16
ALU = mybir.AluOpType
ACT = mybir.ActivationFunctionType
AX = mybir.AxisListType.X

P = 128
C = 128
EPS = 1e-5


def build(nc, x_in, a_wq, a_wkv, a_null, a_wout, f_wq, f_bq, f_wk, f_bk, f_wv, f_bv,
          f_wg1, f_bg1, f_wg2, f_bg2, f_wo, f_bo, out):
    B, T, _ = x_in.shape
    NT = T // P
    HALF = 512
    E = f_wq.shape[0]
    FH = 16
    FD = C // FH
    F_SCALE = float(FD) ** -0.5
    UNITS = B * FH
    NB = 4
    SHIFT = 6
    AH, AD = 16, a_wkv.shape[1]
    PAIRS = AH // 2
    A_SCALE = float(AD) ** -0.5
    KEYS = T + 1
    RING = 8
    A_LAG = 4
    MASKED = -1e30

    with ExitStack() as ctx:
        def sb(name, shape, dt=F32):
            return ctx.enter_context(nc.sbuf_tensor(name, shape, dt))

        def sem(name):
            return ctx.enter_context(nc.semaphore(name))

        q_parts_dram = nc.dram_tensor("q_parts_dram", [UNITS, 3, FD, T], BF16)
        k_parts_dram = nc.dram_tensor("k_parts_dram", [UNITS, 3, FD, T], BF16)
        o_dram = nc.dram_tensor("o_dram", [UNITS, FD, 2, 4, HALF], F32)

        x = sb("x", [P, B * NT, C])
        xn = sb("xn", [P, NT, C])
        xnT = sb("xnT", [P, B, T])
        stats = sb("stats", [P, B * NT, 6])
        mean_var = sb("mean_var", [P, B * NT, 2])
        rstd = sb("rstd", [P, B * NT])
        ident = sb("ident", [P, P])
        eps_col = sb("eps_col", [P, 1])

        w_experts = sb("w_experts", [P, E, 4, C])
        w_mix = sb("w_mix", [P, B, 4, C])
        b_experts = sb("b_experts", [P, 2, E])
        b_mix = sb("b_mix", [P, B, 2])
        wg1 = sb("wg1", [P, C])
        wg2 = sb("wg2", [P, E])
        bg1 = sb("bg1", [P, 1])
        bg2 = sb("bg2", [P, E])
        wo = sb("wo", [P, C])
        bo = sb("bo", [P, C])
        wo_last = sb("wo_last", [P, C])
        tok_sum = sb("tok_sum", [P, B, 2])
        hid = sb("hid", [P, P])
        tri = sb("tri", [P, E, E])
        lg = sb("lg", [P, E])
        g_cmp = sb("g_cmp", [P, E, E])
        g_eq = sb("g_eq", [P, E, E])
        g_s = sb("g_s", [P, 8, E])
        gate = sb("gate", [P, B, E])

        neg_max = sb("neg_max", [P, NB, NT])
        max_parts = sb("max_parts", [P, 32], BF16)
        max_T = sb("max_T", [P, 32], BF16)

        wkv2 = sb("wkv2", [P, 2, AD])
        wout = sb("wout", [P, PAIRS, C])
        null_col = sb("null_col", [P, 1])
        null_sel = sb("null_sel", [P, PAIRS * AH])
        null_out = sb("null_out", [AH, C])
        ident_bf = sb("ident_bf", [P, P], BF16)
        causal = sb("causal", [P, P], BF16)
        wq_pair = sb("wq_pair", [P, 2, 2 * AD])
        a_neg_max = sb("a_neg_max", [P, 2 * NT])
        a_sum = sb("a_sum", [P, 2 * NT])
        a_rsum = sb("a_rsum", [P, 2 * NT])
        p0 = sb("p0", [P, B, NT, AH])
        p0_T = sb("p0_T", [AH, T])

        ARENA = 158 * 256 + 64
        arena = sb("arena", [P, ARENA])
        at = [0]

        def carve(shape, dt=F32):
            n = 1
            for k in shape:
                n *= k
            words = n if dt == F32 else (n + 1) // 2
            flat = arena[:, at[0]:at[0] + words]
            at[0] += words
            assert at[0] <= ARENA, at[0]
            if dt != F32:
                flat = flat.bitcast(dt)[:, 0:n]
            if len(shape) == 1:
                return flat
            names = "abcdef"[:len(shape)]
            return flat.rearrange(f"p ({' '.join(names)}) -> p {' '.join(names)}", **dict(zip(names, shape)))

        k_a = carve([B, KEYS + 1], BF16)
        k_b = carve([B, KEYS + 1], BF16)
        av = carve([B, NT, AD])
        q_part = carve([3, T], BF16)
        q_rest = carve([T])
        Q_S_AT = at[0]
        q_s = carve([2, 2, 3, T], BF16)
        a_probs = carve([RING, KEYS + 3])
        PROBS_T_AT = at[0]
        probs_T = [carve([2, 4 * (qh + 1), HALF]) for qh in range(2)]
        o_T = carve([PAIRS, T])
        at[0] = PROBS_T_AT
        kvf = carve([KEYS + 1])
        kvr = carve([KEYS + 1])
        at[0] = 0
        qkf = carve([2, T])
        qkr = carve([2, T])
        at[0] = Q_S_AT
        q_stack = carve([NB, T], BF16)
        k_stack = carve([NB, T], BF16)
        v_unit = carve([NB, NT, 32])
        parts = carve([2, 3, T], BF16)
        v_all = carve([UNITS, NT, FD])
        o_unit = carve([2, HALF])
        o_last = carve([4, T // 4])
        num_last = carve([T // 4])
        den_last = carve([T // 4])
        ytmp = carve([4, C])
        assert at[0] <= PROBS_T_AT
        at[0] = PROBS_T_AT
        probs = carve([2 * NT, HALF])
        o_all = carve([B, 2, 2, T])
        num = carve([B, T])
        den = carve([B, T])

        ps = ctx.enter_context(nc.psum_tensor("ps", [P, 8, HALF], F32))
        EXP_BANK = [0, 1, 2] * 5 + [1]
        MAX_BANK = [3, 5]
        PV_BANK = 7
        S_BANK = [3, 0]
        GATE_BANK = [6, 1]
        Y_BANK = [0, 1, 5, 6]
        T_BANK = [5, 6]

        w_loaded = sem("w_loaded")
        wo_loaded = sem("wo_loaded")
        aw_loaded = sem("aw_loaded")
        wq_loaded = [sem(f"wq_loaded_{k}") for k in range(2)]
        act_waited = sem("act_waited")
        kv_done = sem("kv_done")
        av_done = sem("av_done")
        av_ready = sem("av_ready")
        kvf_ready = sem("kvf_ready")
        kvr_ready = sem("kvr_ready")
        k_split = sem("k_split")
        k3_ready = sem("k3_ready")
        keys_ready = sem("keys_ready")
        proj_done = sem("proj_done")
        q1_ready = sem("q1_ready")
        q2_ready = sem("q2_ready")
        q3_ready = sem("q3_ready")
        pv_bank_free = sem("pv_bank_free")
        q_s_loaded = [sem(f"q_s_loaded_{k}") for k in range(2)]
        a_scores = sem("a_scores")
        a_max = sem("a_max")
        a_exp = sem("a_exp")
        a_rsum_ready = sem("a_rsum_ready")
        p0_ready = sem("p0_ready")
        a_normed = sem("a_normed")
        tr_done = [sem(f"tr_done_{k}") for k in range(2)]
        evac_dve = sem("evac_dve")
        evac_act = sem("evac_act")
        apv_done = sem("apv_done")
        p0T_done = sem("p0T_done")
        p0T_ready = sem("p0T_ready")
        null_done = sem("null_done")
        null_ready = sem("null_ready")
        ay_done = sem("ay_done")
        x_loaded = [sem(f"x_loaded_{b}") for b in range(B)]
        const_ready = sem("const_ready")
        eps_ready = sem("eps_ready")
        dve_link = sem("dve_link")
        mv_ready = sem("mv_ready")
        std_ready = sem("std_ready")
        xn_ready = sem("xn_ready")
        xT_done = sem("xT_done")
        xnT_ready = sem("xnT_ready")
        hid_done = sem("hid_done")
        hid_ready = sem("hid_ready")
        logits_done = sem("logits_done")
        gexp_in = sem("gexp_in")
        gexp_out = sem("gexp_out")
        mix_ready = sem("mix_ready")
        qk_done = sem("qk_done")
        vproj_done = sem("vproj_done")
        qkf_ready = sem("qkf_ready")
        v_ready = sem("v_ready")
        part1_ready = sem("part1_ready")
        rest_ready = sem("rest_ready")
        part2_ready = sem("part2_ready")
        part3_ready = sem("part3_ready")
        parts_stored = sem("parts_stored")
        pool_waited = sem("pool_waited")
        stacks_loaded = [sem(f"stacks_loaded_{g}") for g in range(NB)]
        rows_zeroed = sem("rows_zeroed")
        stacks_clear = sem("stacks_clear")
        v_unit_ready = sem("v_unit_ready")
        max_scores = sem("max_scores")
        max_read = sem("max_read")
        max_T_ready = sem("max_T_ready")
        max_link = sem("max_link")
        max_rows = sem("max_rows")
        scores_done = sem("scores_done")
        probs_ready = sem("probs_ready")
        pv_done = sem("pv_done")
        o_ready = sem("o_ready")
        o_stored = [sem(f"o_stored_{g}") for g in range(2)]
        o_loaded = [sem(f"o_loaded_{b}") for b in range(B)]
        last_loaded = sem("last_loaded")
        last_ready = sem("last_ready")
        y_started = sem("y_started")
        den_ready = sem("den_ready")
        den_rec = sem("den_rec")
        on_ready = [sem(f"on_ready_{b}") for b in range(B)]
        y_done = sem("y_done")
        x_ready = sem("x_ready")
        out_stored = sem("out_stored")

        STEPS = [(qh, hh, 4 * qh + k) for qh in range(2) for hh in range(2) for k in range(4)]
        NS = len(STEPS)
        USES = [[(k, min(4, qt + 1 - k)) for k in range(0, qt + 1, 4)] for _, _, qt in STEPS]
        FIRST_USE = [sum(len(USES[s]) for s in range(t)) for t in range(NS)]
        V0_STEPS = (0, 1)
        Q_STEPS = (3, 6)
        V1_STEPS = (8, 9, 10, 11)
        P0_STEPS = (12, 13)
        Y_STEPS = (13, 14)

        def q_uses(pg, first, h):
            return (2 if first else 4 * pg + 1) + h

        N_USES = sum(len(v) for v in USES)

        HB = FH // NB + 1
        LR = NB * FD
        TB = 2 * NT

        block = ctx.enter_context(nc.Block())

        @block.sync
        def _(sp):
            for b in range(B):
                sp.dma_start(x[:, b * NT:(b + 1) * NT, :], x_in[b].rearrange("(t p) c -> p t c", p=P)).then_inc(x_loaded[b], 16)
            for k, w in enumerate((f_wq, f_wk, f_wv)):
                sp.dma_start(w_experts[:, :, k, :], w.rearrange("e c d -> c e d")).then_inc(w_loaded, 16)
            sp.dma_start(w_experts[:, :, 3, :], f_bv.unsqueeze(0).broadcast_to([P, E, C])).then_inc(w_loaded, 16)
            with nc.allow_non_contiguous_dma(reason="biases onto partitions"):
                sp.dma_start(b_experts[:, 0, :], f_bq.rearrange("e c -> c e")).then_inc(w_loaded, 16)
                sp.dma_start(b_experts[:, 1, :], f_bk.rearrange("e c -> c e")).then_inc(w_loaded, 16)
            sp.dma_start(wg1[:, :], f_wg1).then_inc(w_loaded, 16)
            sp.dma_start(wg2[:, :], f_wg2).then_inc(w_loaded, 16)
            sp.dma_start(bg1[:, :], f_bg1.unsqueeze(1)).then_inc(w_loaded, 16)
            sp.dma_start(bg2[:, :], f_bg2.unsqueeze(0).broadcast_to([P, E])).then_inc(w_loaded, 16)
            sp.dma_start(wo[:, :], f_wo).then_inc(wo_loaded, 16)
            for k in range(4):
                sp.dma_start(wo_last[k * LR:(k + 1) * LR, :], f_wo[P - LR:P, :]).then_inc(wo_loaded, 16)
            sp.dma_start(bo[:, :], f_bo.unsqueeze(0).broadcast_to([P, C])).then_inc(wo_loaded, 16)
            for h in range(2):
                sp.dma_start(wkv2[:, h, :], a_wkv).then_inc(aw_loaded, 16)
                sp.dma_start(null_col[h * AD:(h + 1) * AD, :], a_null.unsqueeze(1)).then_inc(aw_loaded, 16)
            sp.dma_start(wout[:, :, :], a_wout.rearrange("(p q) c -> q p c", q=P)).then_inc(aw_loaded, 16)
            sp.sem_inc(max_rows, 16)

            def store_parts(f, b):
                for i, part_ready in enumerate((part1_ready, part2_ready, part3_ready)):
                    sp.wait_ge(part_ready, 4 * f + 4)
                    for k, dram in enumerate((q_parts_dram, k_parts_dram)):
                        sp.dma_start(dram.ap()[b * FH:(b + 1) * FH, i],
                                     parts[:, k, i, :]).then_inc(parts_stored, 16)

            def load_stacks(g, u, ul, first):
                if not first:
                    sp.wait_ge(scores_done, TB * u - TB * (NB - 1))
                sp.dma_start(q_stack[0:72, g, :],
                             q_parts_dram.ap()[bass.ds(ul, 1)].rearrange("u i d t -> u (i d) t").broadcast_to([3, 3 * FD, T])
                             ).then_inc(stacks_loaded[g], 16)
                for j in range(3):
                    sp.dma_start(k_stack[24 * j:24 * j + 24, g, :],
                                 k_parts_dram.ap()[bass.ds(ul, 1), j].broadcast_to([3, FD, T])).then_inc(stacks_loaded[g], 16)

            def store_o(g, u, ul):
                sp.wait_ge(o_ready, u + 1)
                for q in range(4):
                    sp.dma_start(o_dram.ap()[bass.ds(ul, 1), :, :, q, :].rearrange("u d k c -> (u d k) c"),
                                 o_unit[32 * q:32 * q + 2 * FD, g % 2, :]).then_inc(o_stored[g % 2], 16)

            def max_rows_in(g, u):
                sp.wait_ge(max_T_ready, u + 1)
                for part in range(2):
                    for blk in range(4):
                        sp.dma_start(
                            q_stack[96 + part:97 + part, g, :].rearrange("p (t b c) -> p t b c", t=NT, b=4)[:, :, blk, :],
                            max_T[32 * blk + NT * part:32 * blk + NT * part + NT, :]).then_inc(max_rows, 16)

            def ffn(ph):
                for b in range(B):
                    store_parts(ph * B + b, b)
                    sp.wait_ge(parts_stored, 96 * (B * ph + b + 1))
                    if b == 0:
                        sp.wait_ge(stacks_clear, 5 * ph + 4)
                        for g in range(NB):
                            load_stacks(g, ph * UNITS + g, g, ph == 0)
                max_rows_in(0, ph * UNITS)

                def load_o(b, u0, u1, stored):
                    for par in range(2):
                        sp.wait_ge(o_stored[par], 32 * UNITS * ph + 64 * ((stored + 1 - par) // 2))
                    sp.dma_start(o_all[(u0 - b * FH) * FD:(u1 - b * FH) * FD, b].rearrange("p k a t -> p (k a t)"),
                                 o_dram.ap()[u0:u1].rearrange("u d k q c -> (u d) (k q c)")).then_inc(o_loaded[b], 16)

                def body(ul, first, last):
                    for g in range(NB):
                        u = ph * UNITS + ul + g
                        if not (last and g == NB - 1):
                            max_rows_in((g + 1) % NB, u + 1)
                        if isinstance(ul, int) and ul == HB * NB and g == 0:
                            load_o(0, 0, FH, ul - 1)
                        if last and g == 1:
                            load_o(1, FH, UNITS - NB, ul)
                        if not (first and g == 0):
                            store_o((g - 1) % NB, u - 1, ul + g - 1)
                        if not last:
                            load_stacks(g, u + NB, ul + g + NB, False)
                body(0, True, False)
                with sp.Fori(1, HB) as i:
                    body(i * NB, False, False)
                for i in range(HB, UNITS // NB):
                    body(i * NB, False, i == UNITS // NB - 1)
                store_o(NB - 1, (ph + 1) * UNITS - 1, UNITS - 1)
                for par in range(2):
                    sp.wait_ge(o_stored[par], 32 * UNITS * (ph + 1))
                for k in range(4):
                    s = slice((k % 2) * (T // 4), (k % 2 + 1) * (T // 4))
                    sp.dma_start(o_last[k * LR:(k + 1) * LR, :, :],
                                 o_dram.ap()[UNITS - NB:UNITS].rearrange("u d k q c -> (u d) (k q) c")[:, k // 2::2, s]
                                 ).then_inc(last_loaded, 16)

            def load_wq(par, pg, pl):
                if not isinstance(pg, int) or pg >= 2:
                    sp.wait_ge(proj_done, 2 * pg - 2)
                sp.dma_start(wq_pair[:, par, :], a_wq[:, bass.ds(pl * 2 * AD, 2 * AD)]).then_inc(wq_loaded[par], 16)

            def build_q_s(par, pg):
                sp.wait_ge(q3_ready, 2 * pg + 2)
                if not isinstance(pg, int) or pg >= 2:
                    sp.wait_ge(a_scores, NS * pg - NS)
                for hh in range(2):
                    rows = slice(hh * AD, (hh + 1) * AD)
                    sp.dma_start(q_s[AD:P, par, hh, :, :], q_part[rows, :, :]).then_inc(q_s_loaded[par], 16)
                    sp.dma_start(q_s[0:AD, par, hh, 0:2, :], q_part[rows, 0:2, :]).then_inc(q_s_loaded[par], 16)
                    sp.dma_start(q_s[0:AD, par, hh, 2, :], q_part[rows, 0, :]).then_inc(q_s_loaded[par], 16)

            def attention():
                for k in range(2):
                    load_wq(k, k, k)
                build_q_s(0, 0)

                def body(b, pl, last):
                    for k in range(2):
                        pg = b * PAIRS + pl + k
                        if not (last and k == 1):
                            build_q_s((k + 1) % 2, pg + 1)
                        if not last:
                            nxt = pl + k + 2
                            load_wq(k, pg + 2, nxt % PAIRS if isinstance(nxt, int) else nxt)
                for b in range(B):
                    body(b, 0, False)
                    with sp.Fori(1, PAIRS // 2 - 1) as i:
                        body(b, i * 2, False)
                    body(b, PAIRS - 2, b == B - 1)

            ffn(0)
            attention()
            ffn(1)
            for b in range(B):
                for g in range(2):
                    sp.wait_ge(x_ready, 4 * B + 2 * b + g + 1)
                    sp.dma_start(out[b].rearrange("(t p) c -> p t c", p=P)[:, 4 * g:4 * g + 4, :],
                                 x[:, b * NT + 4 * g:b * NT + 4 * g + 4, :]).then_inc(out_stored, 16)
            sp.wait_ge(out_stored, 32 * B)

        @block.gpsimd
        def _(pool):
            nc.gpsimd.memset(ident[:, :], 1.0).then_inc(const_ready, 1)
            nc.gpsimd.memset(tri[:, :, :], 1.0).then_inc(const_ready, 1)
            pool.wait_ge(const_ready, 2)
            nc.gpsimd.affine_select(out=ident[:, :], in_=ident[:, :], compare_op=ALU.is_equal, fill=0.0, base=0,
                                    pattern=[[-1, P]], channel_multiplier=1).then_inc(const_ready, 1)
            nc.gpsimd.affine_select(out=tri[:, :, :], in_=tri[:, :, :], compare_op=ALU.is_ge, fill=0.0, base=-1,
                                    pattern=[[1, E], [-1, E]], channel_multiplier=0).then_inc(const_ready, 1)
            nc.gpsimd.memset(max_parts[:, :], 0.0).then_inc(const_ready, 1)
            pool.wait_ge(const_ready, 5)

            def wait(semaphore, value):
                pool.wait_ge(semaphore, value)
                pool.sem_inc(pool_waited, 1)

            nc.gpsimd.memset(causal[:, :], 0.0).then_inc(const_ready, 1)
            nc.gpsimd.tensor_copy(ident_bf[:, :], ident[:, :]).then_inc(const_ready, 1)
            nc.gpsimd.memset(null_sel[:, :], 0.0).then_inc(const_ready, 1)
            pool.wait_ge(const_ready, 8)
            nc.gpsimd.affine_select(out=causal[:, :], in_=causal[:, :], compare_op=ALU.is_ge, fill=MASKED, base=0,
                                    pattern=[[-1, P]], channel_multiplier=1).then_inc(const_ready, 1)
            pool.wait_ge(const_ready, 9)

            def split(f):
                for c in range(4):
                    k, s = c // 2, slice((c % 2) * HALF, (c % 2 + 1) * HALF)
                    pool.wait_ge(part1_ready, 4 * f + c + 1)
                    nc.gpsimd.tensor_tensor(qkr[:, k, s], qkf[:, k, s], parts[:, k, 0, s], ALU.subtract).then_inc(rest_ready, 1)
                for c in range(4):
                    k, s = c // 2, slice((c % 2) * HALF, (c % 2 + 1) * HALF)
                    pool.wait_ge(part2_ready, 4 * f + c + 1)
                    nc.gpsimd.tensor_tensor(parts[:, k, 2, s], qkr[:, k, s], parts[:, k, 1, s], ALU.subtract).then_inc(part3_ready, 1)

            def prepare(g, u, ul, first):
                if not first:
                    wait(scores_done, TB * u - TB * (NB - 1))
                    wait(pv_done, NT // 2 * u - NT // 2 * (NB - 1))
                nc.gpsimd.memset(q_stack[96:98, g, :], 0.0).then_inc(rows_zeroed, 1)
                wait(rows_zeroed, u + 1)
                nc.gpsimd.tensor_copy(v_unit[:, g, :, 0:2 * FD:2],
                                      v_all[:, bass.ds(ul, 1), :, :].rearrange("p u k d -> p (u k) d")).then_inc(v_unit_ready, 1)
                wait(v_unit_ready, u + 1)

            def clear_stacks(ph):
                if ph:
                    pool.wait_ge(a_scores, NS * PAIRS * B)
                nc.gpsimd.memset(q_stack[:, :, :], 0.0).then_inc(stacks_clear, 1)
                nc.gpsimd.memset(k_stack[:, :, :], 0.0).then_inc(stacks_clear, 1)
                nc.gpsimd.memset(v_unit[:, :, :, :], 0.0).then_inc(stacks_clear, 1)
                pool.wait_ge(stacks_clear, 5 * ph + 3)
                nc.gpsimd.memset(k_stack[96:98, :, :], 1.0).then_inc(stacks_clear, 1)
                pool.wait_ge(stacks_clear, 5 * ph + 4)
                nc.gpsimd.memset(v_unit[:, :, :, 1:2 * FD:2], 1.0).then_inc(stacks_clear, 1)
                pool.wait_ge(stacks_clear, 5 * ph + 5)

            def ffn(ph):
                clear_stacks(ph)
                if ph == 0:
                    pool.wait_ge(aw_loaded, 16 * 5)
                    for h in range(2):
                        nc.gpsimd.tensor_copy(null_sel[h * AD:(h + 1) * AD, h:h + (PAIRS - 1) * (AH + 2) + 1:AH + 2],
                                              null_col[h * AD:(h + 1) * AD, :].broadcast_to([AD, PAIRS])).then_inc(const_ready, 1)
                        pool.wait_ge(const_ready, 10 + h)
                for b in range(B):
                    split(ph * B + b)
                    if b == 0:
                        pool.wait_ge(part3_ready, 4 * (ph * B + 1))
                        pool.wait_ge(v_ready, 2 * (ph * B + 1))
                        for g in range(NB - 1):
                            prepare(g, ph * UNITS + g, g, ph == 0)
                pool.wait_ge(part3_ready, 4 * B * (ph + 1))
                pool.wait_ge(v_ready, 2 * B * (ph + 1))

                def sums():
                    pool.wait_ge(o_loaded[0], 16 * (ph + 1))
                    for g in range(2):
                        s = slice(g * HALF, (g + 1) * HALF)
                        for kind, total in ((1, den), (0, num)):
                            nc.gpsimd.tensor_tensor(total[:, 0, s], o_all[:, 0, kind, 0, s], o_all[:, 0, kind, 1, s],
                                                    ALU.add).then_inc(den_ready, 1)
                    pool.wait_ge(den_ready, 4 * (ph + 1))

                def body(ul, last):
                    for g in range(NB):
                        if not last or g == 0:
                            prepare((g - 1) % NB, ph * UNITS + ul + g - 1 + NB, ul + g - 1 + NB, False)
                        if isinstance(ul, int) and ul == HB * NB and g == 1:
                            sums()
                body(0, False)
                with pool.Fori(1, HB) as i:
                    body(i * NB, False)
                for i in range(HB, UNITS // NB):
                    body(i * NB, i == UNITS // NB - 1)
                for g in range(2):
                    s = slice(g * HALF, (g + 1) * HALF)
                    pool.wait_ge(den_rec, 2 * ph + g + 1)
                    nc.gpsimd.tensor_tensor(num[:, 0, s], num[:, 0, s], den[:, 0, s], ALU.mult).then_inc(on_ready[0], 1)

            def q_third(pg, h):
                s = slice(h * HALF, (h + 1) * HALF)
                wait(q2_ready, 2 * pg + h + 1)
                nc.gpsimd.tensor_tensor(q_part[:, 2, s], q_rest[:, s], q_part[:, 1, s], ALU.subtract).then_inc(q3_ready, 1)
                wait(q3_ready, 2 * pg + h + 1)

            def normalize(pg, t):
                n = 1 + (STEPS[t][2] + 1) * P
                wait(a_rsum_ready, NS * pg + t + 1)
                nc.gpsimd.tensor_scalar(a_probs[:, t % RING, 1:n], a_probs[:, t % RING, 1:n], a_rsum[:, t:t + 1], 1.0,
                                        ALU.mult, ALU.mult).then_inc(a_normed, 1)
                wait(a_normed, NS * pg + t + 1)

            def attention():
                for h in range(2):
                    q_third(0, h)

                def body(pg, last):
                    for k in range(2):
                        for t in range(NS):
                            normalize(pg + k, t)
                            if t in Q_STEPS and not (last and k == 1):
                                q_third(pg + k + 1, Q_STEPS.index(t))
                with pool.Fori(0, B * PAIRS // 2 - 1) as i:
                    body(i * 2, False)
                body(B * PAIRS - 2, True)

            ffn(0)
            attention()
            ffn(1)

        @block.scalar
        def _(act):
            act.wait_ge(eps_ready, 1)
            act.sem_inc(probs_ready, TB)

            def norm_std(n, b):
                act.wait_ge(mv_ready, n + 1)
                nc.scalar.activation(rstd[:, b * NT:(b + 1) * NT], mean_var[:, b * NT:(b + 1) * NT, 1], ACT.Sqrt,
                                     bias=eps_col[:, 0:1]).then_inc(std_ready, 1)

            def norm_T(n, b, bank=0):
                for h in range(2):
                    act.wait_ge(xT_done, 2 * n + h + 1)
                    nc.scalar.activation(xnT[:, b, h * HALF:(h + 1) * HALF], ps[:, bank + h, :], ACT.Copy,
                                         accum_out=tok_sum[:, b, h:h + 1]).then_inc(xnT_ready, 1)

            def hidden(f):
                act.wait_ge(hid_done, f + 1)
                nc.scalar.activation(hid[:, :], ps[:, GATE_BANK[f % 2], 0:1].to_broadcast([P, P]), ACT.Relu, bias=bg1[:, 0:1],
                                     scale=1.0 / T).then_inc(hid_ready, 1)

            def gate_exp(f):
                act.wait_ge(gexp_in, f + 1)
                nc.scalar.activation(g_s[:, 1, :], g_s[:, 0, :], ACT.Exp).then_inc(gexp_out, 1)

            def split(f):
                for c in range(4):
                    k, s = c // 2, slice((c % 2) * HALF, (c % 2 + 1) * HALF)
                    act.wait_ge(qkf_ready, 4 * f + c + 1)
                    if f:
                        act.wait_ge(parts_stored, 96 * f)
                    nc.scalar.activation(parts[:, k, 0, s], qkf[:, k, s], ACT.Copy).then_inc(part1_ready, 1)
                for c in range(4):
                    k, s = c // 2, slice((c % 2) * HALF, (c % 2 + 1) * HALF)
                    act.wait_ge(rest_ready, 4 * f + c + 1)
                    nc.scalar.activation(parts[:, k, 1, s], qkr[:, k, s], ACT.Copy).then_inc(part2_ready, 1)

            def wait(semaphore, value):
                act.wait_ge(semaphore, value)
                act.sem_inc(act_waited, 1)

            def values_out(b):
                act.wait_ge(av_done, b + 1)
                nc.scalar.activation(av[:, b, :, :].rearrange("p t d -> p (t d)"), ps[:, 4, :], ACT.Copy).then_inc(av_ready, 1)

            def key_part(b, k):
                if k == 0:
                    act.wait_ge(kvf_ready, b + 1)
                    nc.scalar.activation(k_b[:, b, 0:KEYS], kvf[:, 0:KEYS], ACT.Copy).then_inc(k_split, 1)
                elif k == 1:
                    act.wait_ge(kvr_ready, b + 1)
                    nc.scalar.activation(k_a[:, b, 0:KEYS], kvr[:, 0:KEYS], ACT.Copy).then_inc(k_split, 1)
                else:
                    act.wait_ge(k3_ready, b + 1)
                    nc.scalar.activation(k_a[0:AD, b, 0:KEYS], kvf[0:AD, 0:KEYS], ACT.Copy).then_inc(keys_ready, 1)

            def q_first(pg, par, h):
                if h == 0 and (not isinstance(pg, int) or pg >= 1):
                    act.wait_ge(q_s_loaded[1 - par], 48 * (pg - 1 - (1 - par)) + 96)
                act.wait_ge(proj_done, 2 * pg + h + 1)
                nc.scalar.activation(q_part[:, 0, h * HALF:(h + 1) * HALF], ps[:, PV_BANK, :], ACT.Copy,
                                     scale=A_SCALE).then_inc(q1_ready, 1)

            def q_second(pg, h, k):
                act.wait_ge(pv_bank_free, k + 1)
                nc.scalar.activation(q_part[:, 1, h * HALF:(h + 1) * HALF], q_rest[:, h * HALF:(h + 1) * HALF],
                                     ACT.Copy).then_inc(q2_ready, 1)

            def a_exps(pg, t):
                qh, hh, qt = STEPS[t]
                n = 1 + (qt + 1) * P
                act.wait_ge(a_max, NS * pg + t + 1)
                if t >= RING or not isinstance(pg, int) or pg >= 1:
                    before, pair = (t - RING, pg) if t >= RING else (NS + t - RING, pg - 1)
                    use = FIRST_USE[before] + len(USES[before]) - 1
                    act.wait_ge(tr_done[use % 2], N_USES // 2 * pair + use // 2 + 1)
                nc.scalar.activation(a_probs[:, t % RING, 0:n],
                                     ps[:, S_BANK[t % 2]:S_BANK[t % 2] + (n + HALF - 1) // HALF, :].rearrange("p a b -> p (a b)")[:, 0:n],
                                     ACT.Exp, bias=a_neg_max[:, t:t + 1], accum_out=a_sum[:, t:t + 1]).then_inc(a_exp, 1)

            def a_evac(pg, t):
                qh, hh, qt = STEPS[t]
                for k, (kt, m) in enumerate(USES[t]):
                    use = FIRST_USE[t] + k
                    if use % 2 == 1:
                        act.wait_ge(tr_done[1], N_USES // 2 * pg + use // 2 + 1)
                        nc.scalar.activation(probs_T[qh][:, hh, kt:kt + m, (qt % 4) * P:(qt % 4 + 1) * P],
                                             ps[:, T_BANK[1], 0:m * P].rearrange("p (k q) -> p k q", q=P), ACT.Copy).then_inc(evac_act, 1)

            def p0_evac(b, h, bank):
                act.wait_ge(p0T_done, 2 * b + h + 1)
                if b and h == 0:
                    act.wait_ge(ay_done, 2 * b)
                nc.scalar.activation(p0_T[:, h * HALF:(h + 1) * HALF], ps[0:AH, bank, :], ACT.Copy).then_inc(p0T_ready, 1)

            def attention():
                norm_std(B, 0)
                norm_T(B, 0, 5)
                q_first(0, 0, 0)
                values_out(0)
                key_part(0, 0)
                q_second(0, 0, 0)
                q_first(0, 0, 1)
                key_part(0, 1)
                q_second(0, 1, 1)
                key_part(0, 2)
                for b in range(1, B):
                    norm_std(B + b, b)
                    norm_T(B + b, b, 5)
                    values_out(b)
                    for k in range(3):
                        key_part(b, k)
                act.wait_ge(null_done, 1)
                nc.scalar.activation(null_out[:, :], ps[0:AH, 5, 0:C], ACT.Copy).then_inc(null_ready, 1)

                def body(b, pl, switch, first, last):
                    for k in range(2):
                        pg = b * PAIRS + pl + k
                        turn = switch and k == 0
                        for t in range(NS):
                            if turn and t - 1 in P0_STEPS:
                                p0_evac(b - 1, P0_STEPS.index(t - 1), PV_BANK)
                            if t >= A_LAG:
                                a_evac(pg, t - A_LAG)
                            elif not (first and k == 0):
                                a_evac(pg - 1, NS + t - A_LAG)
                            if t - 1 in Q_STEPS and not (last and k == 1):
                                q_first(pg + 1, (k + 1) % 2, Q_STEPS.index(t - 1))
                            a_exps(pg, t)
                            if t - 1 in Q_STEPS and not (last and k == 1):
                                h = Q_STEPS.index(t - 1)
                                q_second(pg + 1, h, q_uses(pg, first and k == 0, h))
                for b in range(B):
                    body(b, 0, b > 0, b == 0, False)
                    with act.Fori(1, PAIRS // 2 - 1) as i:
                        body(b, i * 2, False, False, False)
                    body(b, PAIRS - 2, False, False, b == B - 1)
                for t in range(NS - A_LAG, NS):
                    a_evac(B * PAIRS - 1, t)
                norm_std(2 * B, 0)
                norm_T(2 * B, 0, 5)
                for h in range(2):
                    p0_evac(B - 1, h, 2 + h)
                hidden(B)
                gate_exp(B)
                split(B)

            def evacuate(g, u):
                act.wait_ge(pv_done, NT // 2 * u + NT // 2)
                act.wait_ge(o_stored[g % 2], 32 * (u - g % 2))
                nc.scalar.activation(o_unit[:, g % 2, :], ps[:, PV_BANK, :], ACT.Copy).then_inc(o_ready, 1)

            def exps(g, u, first):
                for t in range(TB):
                    act.wait_ge(scores_done, TB * u + t + 1)
                    if t % 4 == 0 and not first:
                        act.wait_ge(pv_done, NT // 2 * u - NT // 2 + t // 4 + 1)
                    nc.scalar.activation(probs[:, t, :], ps[:, EXP_BANK[t], :], ACT.Exp, scale=F_SCALE).then_inc(probs_ready, 1)
                    if t == 4 and not first:
                        evacuate((g - 1) % NB, u - 1)

            def ffn(ph):
                if ph == 0:
                    norm_std(0, 0)
                    norm_std(1, 1)
                    norm_T(0, 0)
                    hidden(0)
                    gate_exp(0)
                else:
                    norm_std(2 * B + 1, 1)
                norm_T(2 * ph * B + 1, 1)
                hidden(ph * B + 1)
                if ph == 0:
                    split(0)
                gate_exp(ph * B + 1)
                split(ph * B + 1)

                def body(ul, first):
                    for g in range(NB):
                        exps(g, ph * UNITS + ul + g, first and g == 0)
                body(0, True)
                with act.Fori(1, UNITS // NB) as i:
                    body(i * NB, False)
                evacuate(NB - 1, ph * UNITS + UNITS - 1)

            ffn(0)
            attention()
            ffn(1)

        @block.vector
        def _(dve):
            made = [0]

            def link(ins):
                made[0] += 1
                ins.then_inc(dve_link, 1)
                dve.wait_ge(dve_link, made[0])

            nc.vector.memset(eps_col[:, :], EPS).then_inc(eps_ready, 1)
            dve.sem_inc(max_read, 2)

            def norm(n, b):
                if n < B:
                    dve.wait_ge(x_loaded[b], 16)
                else:
                    dve.wait_ge(x_ready, 2 * (n - B) + 2)
                for t in range(b * NT, (b + 1) * NT):
                    ins = nc.vector.bn_stats(stats[:, t, :], x[:, t, :])
                link(ins)
                for t in range(b * NT, (b + 1) * NT):
                    ins = nc.vector.bn_aggr(mean_var[:, t, :], stats[:, t, :])
                ins.then_inc(mv_ready, 1)
                dve.wait_ge(std_ready, n + 1)
                if n:
                    dve.wait_ge(xT_done, 2 * n)
                link(nc.vector.reciprocal(rstd[:, b * NT:(b + 1) * NT], rstd[:, b * NT:(b + 1) * NT]))
                for t in range(b * NT, (b + 1) * NT):
                    ins = nc.vector.tensor_scalar(xn[:, t % NT, :], x[:, t, :], mean_var[:, t, 0:1], rstd[:, t:t + 1],
                                                  ALU.subtract, ALU.mult)
                    if t % 4 == 3:
                        ins.then_inc(xn_ready, 1)

            def gating(f, b):
                dve.wait_ge(logits_done, f + 1)
                if f == 0:
                    dve.wait_ge(w_loaded, 16 * 10)
                    dve.wait_ge(const_ready, 5)
                link(nc.vector.tensor_tensor(lg[:, :], ps[:, GATE_BANK[b], 8:8 + E], bg2[:, :], ALU.add))
                other = lg[:, :].unsqueeze(1).broadcast_to([P, E, E])
                own = lg[:, :].unsqueeze(2).broadcast_to([P, E, E])
                nc.vector.tensor_tensor(g_cmp[:, :, :], other, own, ALU.is_gt)
                link(nc.vector.tensor_tensor(g_eq[:, :, :], other, own, ALU.is_equal))
                link(nc.vector.tensor_tensor(g_eq[:, :, :], g_eq[:, :, :], tri[:, :, :], ALU.mult))
                link(nc.vector.tensor_tensor(g_cmp[:, :, :], g_cmp[:, :, :], g_eq[:, :, :], ALU.add))
                nc.vector.reduce_sum(g_s[:, 2, :], g_cmp[:, :, :], AX)
                link(nc.vector.reduce_max(g_s[:, 3, 0:1], lg[:, :], AX))
                link(nc.vector.tensor_scalar(g_s[:, 4, :], g_s[:, 2, :], 1.5, None, ALU.is_lt))
                nc.vector.tensor_scalar(g_s[:, 0, :], lg[:, :], g_s[:, 3, 0:1], None, ALU.subtract).then_inc(gexp_in, 1)
                dve.wait_ge(gexp_out, f + 1)
                link(nc.vector.tensor_tensor(g_s[:, 5, :], g_s[:, 1, :], g_s[:, 4, :], ALU.mult))
                link(nc.vector.reduce_sum(g_s[:, 6, 0:1], g_s[:, 5, :], AX))
                link(nc.vector.reciprocal(g_s[:, 7, 0:1], g_s[:, 6, 0:1]))
                link(nc.vector.tensor_scalar(gate[:, b, :], g_s[:, 5, :], g_s[:, 7, 0:1], None, ALU.mult))
                wm = w_mix[:, b].rearrange("p k d -> p (k d)")
                bm = b_mix[:, b, :]
                for e in range(E):
                    we = w_experts[:, e].rearrange("p k d -> p (k d)")
                    be = b_experts[:, :, e]
                    ge = gate[:, b, e:e + 1]
                    if e == 0:
                        nc.vector.tensor_scalar(bm, be, ge, None, ALU.mult)
                        link(nc.vector.tensor_scalar(wm, we, ge, None, ALU.mult))
                    else:
                        nc.vector.scalar_tensor_tensor(bm, be, ge, bm, ALU.mult, ALU.add)
                        ins = nc.vector.scalar_tensor_tensor(wm, we, ge, wm, ALU.mult, ALU.add)
                        if e < E - 1:
                            link(ins)
                        else:
                            ins.then_inc(mix_ready, 1)

            def project(f, b):
                dve.wait_ge(mix_ready, f + 1)
                for c in range(4):
                    k, s = c // 2, slice((c % 2) * HALF, (c % 2 + 1) * HALF)
                    dve.wait_ge(qk_done, 4 * f + c + 1)
                    if f:
                        dve.wait_ge(rest_ready, 4 * f)
                        dve.wait_ge(part1_ready, 4 * f)
                    nc.vector.tensor_scalar(qkf[:, k, s], ps[:, 2 + c, :], b_mix[:, b, k:k + 1], None, ALU.add).then_inc(qkf_ready, 1)
                for g in range(2):
                    dve.wait_ge(vproj_done, 2 * f + g + 1)
                    for t in range(4):
                        ins = nc.vector.tensor_tensor(
                            v_all[:, b * FH:(b + 1) * FH, 4 * g + t, :],
                            ps[:, 6 + g, t * C:(t + 1) * C].rearrange("p (h d) -> p h d", d=FD),
                            w_mix[:, b, 3, :].rearrange("p (h d) -> p h d", d=FD), ALU.add)
                    ins.then_inc(v_ready, 1)

            def maxima(g, u):
                for t in range(NT):
                    dve.wait_ge(max_scores, NT * u + t + 1)
                    bank = MAX_BANK[t % 2]
                    nc.vector.tensor_reduce(neg_max[:, g, t:t + 1], ps[:, bank:bank + 2, :].rearrange("p a b -> p (a b)"), AX,
                                            ALU.max, negate=True).then_inc(max_read, 1)
                dve.wait_ge(max_read, 2 + NT * u + NT)
                nc.vector.tensor_copy(max_parts[:, 0:NT], neg_max[:, g, :]).then_inc(max_link, 1)
                dve.wait_ge(max_link, 2 * u + 1)
                nc.vector.tensor_tensor(max_parts[:, NT:2 * NT], neg_max[:, g, :], max_parts[:, 0:NT], ALU.subtract).then_inc(max_link, 1)
                dve.wait_ge(max_link, 2 * u + 2)
                dve.wait_ge(max_rows, 128 * u + 16)
                nc.vector.transpose(max_T[:, :], max_parts[:, :]).then_inc(max_T_ready, 1)

            def recip_0(ph, g):
                dve.wait_ge(den_ready, 4 * (ph + 1))
                s = slice(g * HALF, (g + 1) * HALF)
                nc.vector.reciprocal(den[:, 0, s], den[:, 0, s]).then_inc(den_rec, 1)

            def normalize_1(ph, g):
                dve.wait_ge(o_loaded[1], 16 * (ph + 1))
                s, r = slice(g * HALF, (g + 1) * HALF), slice(0, P - LR)
                link(nc.vector.tensor_tensor(den[r, 1, s], o_all[r, 1, 1, 0, s], o_all[r, 1, 1, 1, s], ALU.add))
                nc.vector.tensor_tensor(num[r, 1, s], o_all[r, 1, 0, 0, s], o_all[r, 1, 0, 1, s], ALU.add)
                link(nc.vector.reciprocal(den[r, 1, s], den[r, 1, s]))
                nc.vector.tensor_tensor(num[r, 1, s], num[r, 1, s], den[r, 1, s], ALU.mult).then_inc(on_ready[1], 1)

            def normalize_last(ph):
                dve.wait_ge(last_loaded, 64 * (ph + 1))
                link(nc.vector.tensor_tensor(den_last[:, :], o_last[:, 2, :], o_last[:, 3, :], ALU.add))
                nc.vector.tensor_tensor(num_last[:, :], o_last[:, 0, :], o_last[:, 1, :], ALU.add)
                link(nc.vector.reciprocal(den_last[:, :], den_last[:, :]))
                nc.vector.tensor_tensor(num_last[:, :], num_last[:, :], den_last[:, :], ALU.mult).then_inc(last_ready, 1)

            def finish(f, b):
                dve.wait_ge(wo_loaded, 16 * 6)
                for g in range(2):
                    xs = x[:, b * NT + 4 * g:b * NT + 4 * g + 4, :]
                    dve.wait_ge(y_done, 2 * f + g + 1)
                    n = f if f < B else f + B
                    if 2 * n + g:
                        dve.wait_ge(x_ready, 2 * n + g)
                    if b == 0:
                        y = ps[:, g, :].rearrange("p (a t c) -> p a t c", a=2, c=C)
                    else:
                        y = ps[:, Y_BANK[2 * g]:Y_BANK[2 * g] + 2, 0:2 * C].rearrange("p a (t c) -> p a t c", c=C)
                    nc.vector.tensor_tensor(ytmp[:, :, :].rearrange("p (a t) c -> p a t c", a=2), y,
                                            bo[:, :].unsqueeze(1).unsqueeze(1).broadcast_to([P, 2, 2, C]),
                                            ALU.add).then_inc(dve_link, 1)
                    made[0] += 1
                    dve.wait_ge(dve_link, made[0])
                    nc.vector.scalar_tensor_tensor(xs, ytmp[:, :, :], 0.5, xs, ALU.mult, ALU.add).then_inc(x_ready, 1)

            def keys_in(b):
                if b:
                    dve.wait_ge(keys_ready, b)
                for h in range(2):
                    dve.wait_ge(kv_done, 2 * b + h + 1)
                    ins = nc.vector.tensor_copy(kvf[:, 1 + h * HALF:1 + (h + 1) * HALF], ps[:, 2 + h, :])
                nc.vector.tensor_copy(kvf[:, 0:1], null_col[:, :]).then_inc(kvf_ready, 1)

            def keys_rest(b):
                dve.wait_ge(k_split, 2 * b + 1)
                nc.vector.tensor_tensor(kvr[:, 0:KEYS], kvf[:, 0:KEYS], k_b[:, b, 0:KEYS], ALU.subtract).then_inc(kvr_ready, 1)
                dve.wait_ge(k_split, 2 * b + 2)
                nc.vector.tensor_tensor(k_b[0:AD, b, 0:KEYS], kvr[0:AD, 0:KEYS], k_a[0:AD, b, 0:KEYS], ALU.subtract).then_inc(k3_ready, 1)

            def q_rests(pg, h):
                if h == 0 and (not isinstance(pg, int) or pg >= 1):
                    dve.wait_ge(q3_ready, 2 * pg)
                dve.wait_ge(q1_ready, 2 * pg + h + 1)
                s = slice(h * HALF, (h + 1) * HALF)
                nc.vector.scalar_tensor_tensor(q_rest[:, s], ps[:, PV_BANK, :], A_SCALE, q_part[:, 0, s], ALU.mult,
                                               ALU.subtract).then_inc(pv_bank_free, 1)

            def a_maximum(pg, t):
                n = 1 + (STEPS[t][2] + 1) * P
                dve.wait_ge(a_scores, NS * pg + t + 1)
                nc.vector.tensor_reduce(a_neg_max[:, t:t + 1],
                                        ps[:, S_BANK[t % 2]:S_BANK[t % 2] + (n + HALF - 1) // HALF, :].rearrange("p a b -> p (a b)")[:, 0:n],
                                        AX, ALU.max, negate=True).then_inc(a_max, 1)

            def a_recip(pg, b, pl, t):
                qh, hh, qt = STEPS[t]
                dve.wait_ge(a_exp, NS * pg + t + 1)
                nc.vector.reciprocal(a_rsum[:, t:t + 1], a_sum[:, t:t + 1]).then_inc(a_rsum_ready, 1)
                dve.wait_ge(a_rsum_ready, NS * pg + t + 1)
                nc.vector.tensor_tensor(p0[:, b, qt, bass.ds(2 * pl + hh, 1)], a_probs[:, t % RING, 0:1], a_rsum[:, t:t + 1],
                                        ALU.mult).then_inc(p0_ready, 1)

            def a_evac(pg, t):
                qh, hh, qt = STEPS[t]
                for k, (kt, m) in enumerate(USES[t]):
                    use = FIRST_USE[t] + k
                    if use % 2 == 0:
                        dve.wait_ge(tr_done[0], N_USES // 2 * pg + use // 2 + 1)
                        nc.vector.tensor_copy(probs_T[qh][:, hh, kt:kt + m, (qt % 4) * P:(qt % 4 + 1) * P],
                                              ps[:, T_BANK[0], 0:m * P].rearrange("p (k q) -> p k q", q=P)).then_inc(evac_dve, 1)

            def o_evac(pg, pl, qh):
                dve.wait_ge(apv_done, 2 * pg + qh + 1)
                nc.vector.tensor_scalar(o_T[:, bass.ds(pl, 1), qh * HALF:(qh + 1) * HALF].rearrange("p a b -> p (a b)"),
                                        ps[:, PV_BANK, :], 1.0, None, ALU.mult).then_inc(pv_bank_free, 1)

            def add_out(b, g, bank):
                dve.wait_ge(ay_done, 2 * b + g + 1)
                xs = x[:, b * NT + 4 * g:b * NT + 4 * g + 4, :].rearrange("p t c -> p (t c)")
                nc.vector.tensor_tensor(xs, ps[:, bank, :], xs, ALU.add).then_inc(x_ready, 1)

            def attention():
                keys_rest(0)
                for b in range(1, B):
                    norm(B + b, b)
                    keys_in(b)
                    keys_rest(b)

                def body(b, pl, switch, first, last):
                    for k in range(2):
                        pg = b * PAIRS + pl + k
                        turn = switch and k == 0
                        before = (b - 1, PAIRS - 1) if turn else (b, pl + k - 1)
                        for t in range(NS):
                            a_maximum(pg, t)
                            if t >= A_LAG:
                                a_evac(pg, t - A_LAG)
                            elif not (first and k == 0):
                                a_evac(pg - 1, NS + t - A_LAG)
                            if t >= 2:
                                a_recip(pg, b, pl + k, t - 2)
                            elif not (first and k == 0):
                                a_recip(pg - 1, *before, NS + t - 2)
                            if t - 1 == V0_STEPS[-1] and not (first and k == 0):
                                o_evac(pg - 1, before[1], 0)
                            if t - 1 in Q_STEPS and not (last and k == 1):
                                q_rests(pg + 1, Q_STEPS.index(t - 1))
                            if t - 1 == V1_STEPS[-1] and not (first and k == 0):
                                o_evac(pg - 1, before[1], 1)
                            if turn and t - 1 in Y_STEPS:
                                add_out(b - 1, Y_STEPS.index(t - 1), PV_BANK)
                for b in range(B):
                    body(b, 0, b > 0, b == 0, False)
                    with dve.Fori(1, PAIRS // 2 - 1) as i:
                        body(b, i * 2, False, False, False)
                    body(b, PAIRS - 2, False, False, b == B - 1)
                pg = B * PAIRS - 1
                for t in range(NS - 2, NS):
                    a_recip(pg, B - 1, PAIRS - 1, t)
                o_evac(pg, PAIRS - 1, 0)
                for t in range(NS - A_LAG, NS):
                    a_evac(pg, t)
                norm(2 * B, 0)
                o_evac(pg, PAIRS - 1, 1)
                gating(B, 0)
                add_out(B - 1, 0, 0)
                project(B, 0)
                add_out(B - 1, 1, 1)

            def ffn(ph):
                if ph == 0:
                    norm(0, 0)
                norm(2 * ph * B + 1, 1)
                if ph == 0:
                    gating(0, 0)
                    project(0, 0)
                gating(ph * B + 1, 1)
                project(ph * B + 1, 1)
                with dve.Fori(0, HB) as i:
                    for g in range(NB):
                        maxima(g, ph * UNITS + i * NB + g)
                for i in range(HB, UNITS // NB):
                    for g in range(NB):
                        maxima(g, ph * UNITS + i * NB + g)
                    if i < HB + 2:
                        recip_0(ph, i - HB)
                for g in range(2):
                    normalize_1(ph, g)
                finish(ph * B, 0)
                if ph == 0:
                    norm(B, 0)
                    q_rests(0, 0)
                normalize_last(ph)
                if ph == 0:
                    keys_in(0)
                    q_rests(0, 1)
                finish(ph * B + 1, 1)

            ffn(0)
            attention()
            ffn(1)

        @block.tensor
        def _(pe):
            pe.wait_ge(const_ready, 5)
            pe.wait_ge(w_loaded, 16 * 10)

            def norm_T(n, b, bank=0):
                for h in range(2):
                    pe.wait_ge(xn_ready, 2 * n + h + 1)
                    for t in range(4):
                        ins = nc.tensor.transpose(ps[:, bank + h, t * P:(t + 1) * P], xn[:, 4 * h + t, :], ident[:, :])
                    ins.then_inc(xT_done, 1)

            def gates(n, f, b):
                pe.wait_ge(xnT_ready, 2 * n + 2)
                for h in range(2):
                    ins = nc.tensor.matmul(ps[:, GATE_BANK[b], 0:1], wg1[:, :], tok_sum[:, b, h:h + 1], start=h == 0, stop=h == 1)
                ins.then_inc(hid_done, 1)
                pe.wait_ge(hid_ready, f + 1)
                nc.tensor.matmul(ps[:, GATE_BANK[b], 8:8 + E], hid[:, :], wg2[:, :], start=True, stop=True).then_inc(logits_done, 1)

            def project(f, b):
                pe.wait_ge(mix_ready, f + 1)
                if f:
                    pe.wait_ge(qkf_ready, 4 * f)
                    pe.wait_ge(v_ready, 2 * f)
                for c in range(4):
                    nc.tensor.matmul(ps[:, 2 + c, :], w_mix[:, b, c // 2, :], xnT[:, b, (c % 2) * HALF:(c % 2 + 1) * HALF],
                                     start=True, stop=True).then_inc(qk_done, 1)
                for g in range(2):
                    for t in range(4):
                        ins = nc.tensor.matmul(ps[:, 6 + g, t * C:(t + 1) * C], xnT[:, b, (4 * g + t) * P:(4 * g + t + 1) * P],
                                               w_mix[:, b, 2, :], start=True, stop=True)
                    ins.then_inc(vproj_done, 1)

            def max_tile(g, u, t):
                if t == 0:
                    pe.wait_ge(stacks_loaded[g], 64 // NB * (u - g) + 64)
                    pe.wait_ge(rows_zeroed, u + 1)
                pe.wait_ge(max_read, NT * u + t + 1)
                bank = MAX_BANK[t % 2]
                for h in range(2):
                    ins = nc.tensor.matmul(ps[:, bank + h, :], q_stack[:, g, t * P:(t + 1) * P],
                                           k_stack[:, g, h * HALF:(h + 1) * HALF], start=True, stop=True)
                ins.then_inc(max_scores, 1)

            def score_tile(g, u, kt, h):
                if kt == 0 and h == 0:
                    pe.wait_ge(max_rows, 128 * u + 128 + 16)
                t = 2 * kt + h
                bank = EXP_BANK[t]
                before = max([s for s in range(t) if EXP_BANK[s] == bank] + [max(s for s in range(TB) if EXP_BANK[s] == bank) - TB
                                                                             if t < 3 else -TB])
                pe.wait_ge(probs_ready, TB + TB * u + before + 1)
                ins = nc.tensor.matmul(ps[:, bank, :], k_stack[:, g, kt * P:(kt + 1) * P],
                                       q_stack[:, g, h * HALF:(h + 1) * HALF], start=True, stop=True)
                ins.then_inc(scores_done, 1)

            def values(g, u, j):
                if j == 0:
                    pe.wait_ge(v_unit_ready, u + 1)
                    pe.wait_ge(o_ready, u)
                pe.wait_ge(probs_ready, TB + TB * u + 4 * j + 4)
                for t in range(4 * j, 4 * j + 4):
                    col = 32 * (t % 4)
                    ins = nc.tensor.matmul(ps[col:col + 32, PV_BANK, :], v_unit[:, g, t // 2, :], probs[:, t, :],
                                           start=j == 0, stop=j == NT // 2 - 1)
                ins.then_inc(pv_done, 1)

            LAG = 2

            def unit(g, u, first, ahead):
                for kt in range(NT):
                    score_tile(g, u, kt, 0)
                    if kt < NT - SHIFT and ahead > 0:
                        max_tile((g + 1) % NB, u + 1, SHIFT + kt)
                    elif kt >= NT - SHIFT and ahead > 1:
                        max_tile((g + 2) % NB, u + 2, kt - (NT - SHIFT))
                    score_tile(g, u, kt, 1)
                    if kt % 2 == 1:
                        j = kt // 2 - 1
                        if j >= 0:
                            values(g, u, j)
                        elif not first:
                            values((g - 1) % NB, u - 1, NT // 2 - 1)

            def finish_0(ph):
                pe.wait_ge(wo_loaded, 16 * 6)
                for g in range(2):
                    pe.wait_ge(on_ready[0], 2 * ph + g + 1)
                    for t in range(4):
                        k = 4 * g + t
                        ins = nc.tensor.matmul(ps[:, g, t * C:(t + 1) * C], num[:, 0, k * P:(k + 1) * P], wo[:, :],
                                               start=True, stop=True)
                    ins.then_inc(y_done, 1)

            def finish_1(ph):
                pe.wait_ge(on_ready[1], 2 * ph + 2)
                pe.wait_ge(x_ready, 8 * ph + 2)
                for k in range(NT):
                    ins = nc.tensor.matmul(ps[:, Y_BANK[k // 2], k % 2 * C:(k % 2 + 1) * C], num[0:P - LR, 1, k * P:(k + 1) * P],
                                           wo[0:P - LR, :], start=k % 2 == 0, stop=False, skip_group_check=True)
                ins.then_inc(y_started, 1)

            def finish_last(ph):
                pe.wait_ge(y_started, ph + 1)
                pe.wait_ge(last_ready, ph + 1)
                for k in range(NT):
                    r = slice(k // 2 * LR, (k // 2 + 1) * LR)
                    ins = nc.tensor.matmul(ps[:, Y_BANK[k // 2], k % 2 * C:(k % 2 + 1) * C], num_last[r, (k % 2) * P:(k % 2 + 1) * P],
                                           wo_last[r, :], start=False, stop=k % 2 == 1, skip_group_check=True)
                    if k % 4 == 3:
                        ins.then_inc(y_done, 1)

            def keys(b):
                pe.wait_ge(xnT_ready, 2 * (2 + b) + 2)
                if b:
                    pe.wait_ge(kvf_ready, b)
                    pe.wait_ge(av_ready, b)
                for h in range(2):
                    nc.tensor.matmul(ps[:, 2 + h, :], wkv2[:, :, :].rearrange("p a b -> p (a b)"), xnT[:, b, h * HALF:(h + 1) * HALF],
                                     start=True, stop=True).then_inc(kv_done, 1)
                for t in range(NT):
                    ins = nc.tensor.matmul(ps[:, 4, t * AD:(t + 1) * AD], xnT[:, b, t * P:(t + 1) * P], wkv2[:, 0, :],
                                           start=True, stop=True)
                ins.then_inc(av_done, 1)

            def queries(pg, k, b, par, h):
                if h == 0:
                    pe.wait_ge(wq_loaded[par], 8 * (pg - par) + 16)
                if not isinstance(pg, int) or k > 0:
                    pe.wait_ge(pv_bank_free, k)
                nc.tensor.matmul(ps[:, PV_BANK, :], wq_pair[:, par, :], xnT[:, b, h * HALF:(h + 1) * HALF],
                                 start=True, stop=True).then_inc(proj_done, 1)

            def a_score_tile(pg, b, par, t):
                qh, hh, qt = STEPS[t]
                n = 1 + (qt + 1) * P
                if t == 0:
                    pe.wait_ge(q_s_loaded[par], 48 * (pg - par) + 96)
                if t >= 2 or not isinstance(pg, int) or pg >= 1:
                    pe.wait_ge(a_exp, NS * pg + t - 1)
                cols = slice(qt * P, (qt + 1) * P)
                for c0 in range(0, n, HALF):
                    c1 = min(n, c0 + HALF)
                    m0, m1 = max(c0, 1 + qt * P), c1
                    bank = S_BANK[t % 2] + c0 // HALF
                    passes = [(q_s[:, par, hh, k, cols], key[:, b, c0:c1], 0, c1 - c0) for k, key in enumerate((k_a, k_a, k_b))]
                    if m1 > m0:
                        passes.append((ident_bf[:, :], causal[:, m0 - 1 - qt * P:m1 - 1 - qt * P], m0 - c0, m1 - c0))
                    for k, (lhs, rhs, o0, o1) in enumerate(passes):
                        ins = nc.tensor.matmul(ps[:, bank, o0:o1], lhs, rhs, start=k == 0, stop=k == len(passes) - 1)
                ins.then_inc(a_scores, 1)

            def a_transposes(pg, t):
                qh, hh, qt = STEPS[t]
                pe.wait_ge(a_normed, NS * pg + t + 1)
                for k, (kt, m) in enumerate(USES[t]):
                    use = FIRST_USE[t] + k
                    if use >= 2 or not isinstance(pg, int) or pg >= 1:
                        pe.wait_ge(evac_act if use % 2 else evac_dve, N_USES // 2 * pg + use // 2)
                    for j in range(m):
                        ins = nc.tensor.transpose(ps[:, T_BANK[use % 2], j * P:(j + 1) * P],
                                                  a_probs[:, t % RING, 1 + (kt + j) * P:1 + (kt + j + 1) * P], ident[:, :])
                    ins.then_inc(tr_done[use % 2], 1)

            def a_values(pg, b, qh, k0, part):
                nk = 4 * (qh + 1)
                if part == 0:
                    last = [s for s in range(NS) if STEPS[s][0] == qh][-1]
                    done = (FIRST_USE[last] + len(USES[last])) // 2
                    pe.wait_ge(evac_dve, N_USES // 2 * pg + done)
                    pe.wait_ge(evac_act, N_USES // 2 * pg + done)
                    pe.wait_ge(pv_bank_free, k0)
                for kt in (2 * part, 2 * part + 1):
                    q0 = max(0, kt - 4 * qh) * P
                    for hh in range(2):
                        ins = nc.tensor.matmul(ps[hh * AD:(hh + 1) * AD, PV_BANK, q0:HALF], av[:, b, kt, :],
                                               probs_T[qh][:, hh, kt, q0:HALF], start=kt == 0, stop=kt == nk - 1)
                if kt == nk - 1:
                    ins.then_inc(apv_done, 1)

            def p0_transposes(b, h, bank):
                if h == 0:
                    pe.wait_ge(p0_ready, NS * PAIRS * (b + 1))
                for t in range(4):
                    ins = nc.tensor.transpose(ps[0:AH, bank, t * P:(t + 1) * P], p0[:, b, 4 * h + t, :], ident[:, :])
                ins.then_inc(p0T_done, 1)

            def outputs(b, g, bank):
                for t in range(4):
                    tok = slice((4 * g + t) * P, (4 * g + t + 1) * P)
                    for p in range(PAIRS):
                        nc.tensor.matmul(ps[:, bank, t * C:(t + 1) * C], o_T[:, p, tok], wout[:, p, :], start=p == 0, stop=False)
                    ins = nc.tensor.matmul(ps[:, bank, t * C:(t + 1) * C], p0_T[:, tok], null_out[:, :], start=False, stop=True)
                ins.then_inc(ay_done, 1)

            def attention():
                for b in range(1, B):
                    norm_T(B + b, b, 5)
                    keys(b)
                pe.wait_ge(const_ready, 11)
                pe.wait_ge(xnT_ready, 2 * 2 * B)
                for p in range(PAIRS):
                    ins = nc.tensor.matmul(ps[0:AH, 5, 0:C], null_sel[:, p * AH:(p + 1) * AH], wout[:, p, :],
                                           start=p == 0, stop=p == PAIRS - 1)
                ins.then_inc(null_done, 1)
                pe.wait_ge(keys_ready, B)
                pe.wait_ge(av_ready, B)
                pe.wait_ge(null_ready, 1)

                def body(b, pl, switch, first, last):
                    for k in range(2):
                        pg = b * PAIRS + pl + k
                        turn = switch and k == 0
                        bb = b - 1 if turn else b
                        bn = b + 1 if isinstance(pl, int) and pl + k == PAIRS - 1 else b
                        no_q = last and k == 1
                        for t in range(NS):
                            a_score_tile(pg, b, k, t)
                            if t >= A_LAG:
                                a_transposes(pg, t - A_LAG)
                            elif not (first and k == 0):
                                a_transposes(pg - 1, NS + t - A_LAG)
                            if t in V0_STEPS and not (first and k == 0):
                                if switch and k == 1 and t == V0_STEPS[0]:
                                    pe.wait_ge(x_ready, 2 * B + 2 * b)
                                a_values(pg - 1, bb, 0, 4 * pg, V0_STEPS.index(t))
                            if t in Q_STEPS and not no_q:
                                h = Q_STEPS.index(t)
                                queries(pg + 1, q_uses(pg, first and k == 0, h), bn, (k + 1) % 2, h)
                            if t in V1_STEPS and not (first and k == 0):
                                a_values(pg - 1, bb, 1, 4 * pg + (1 if no_q else 3), V1_STEPS.index(t))
                            if turn and t in P0_STEPS:
                                h = P0_STEPS.index(t)
                                if h == 0:
                                    pe.wait_ge(pv_bank_free, 4 * pg + 4)
                                else:
                                    pe.wait_ge(p0T_ready, 2 * (b - 1) + 1)
                                p0_transposes(b - 1, h, PV_BANK)
                            if turn and t in Y_STEPS:
                                g = Y_STEPS.index(t)
                                if g == 0:
                                    pe.wait_ge(p0T_ready, 2 * b)
                                else:
                                    pe.wait_ge(x_ready, 2 * B + 2 * b - 1)
                                outputs(b - 1, g, PV_BANK)
                for b in range(B):
                    body(b, 0, b > 0, b == 0, False)
                    with pe.Fori(1, PAIRS // 2 - 1) as i:
                        body(b, i * 2, False, False, False)
                    body(b, PAIRS - 2, False, False, b == B - 1)
                pg = B * PAIRS - 1
                for part in range(2):
                    a_values(pg, B - 1, 0, 4 * pg + 2, part)
                for t in range(NS - A_LAG, NS):
                    a_transposes(pg, t)
                for part in range(4):
                    a_values(pg, B - 1, 1, 4 * pg + 3, part)
                norm_T(2 * B, 0, 5)
                pe.wait_ge(a_exp, NS * (pg + 1))
                for h in range(2):
                    p0_transposes(B - 1, h, 2 + h)
                gates(2 * B, B, 0)
                pe.wait_ge(p0T_ready, 2 * B)
                pe.wait_ge(pv_bank_free, 4 * (pg + 1))
                outputs(B - 1, 0, 0)
                project(B, 0)
                outputs(B - 1, 1, 1)

            def ffn(ph):
                if ph == 0:
                    norm_T(0, 0)
                    gates(0, 0, 0)
                norm_T(2 * ph * B + 1, 1)
                gates(2 * ph * B + 1, ph * B + 1, 1)
                if ph == 0:
                    project(0, 0)
                project(ph * B + 1, 1)
                pe.wait_ge(qkf_ready, 4 * B * (ph + 1))
                pe.wait_ge(v_ready, 2 * B * (ph + 1))
                u0 = ph * UNITS
                for t in range(NT):
                    max_tile(0, u0, t)
                for t in range(SHIFT):
                    max_tile(1, u0 + 1, t)
                for g in range(NB):
                    unit(g, u0 + g, g == 0, NB)
                with pe.Fori(1, UNITS // NB - 1) as i:
                    for g in range(NB):
                        unit(g, i * NB + (u0 + g), False, NB)
                for g in range(NB):
                    unit(g, u0 + UNITS - NB + g, False, NB - 1 - g)
                values(NB - 1, u0 + UNITS - 1, NT // 2 - 1)
                finish_0(ph)
                if ph == 0:
                    norm_T(B, 0, 5)
                    pe.wait_ge(xnT_ready, 2 * B + 2)
                    queries(0, 0, 0, 0, 0)
                    keys(0)
                finish_1(ph)
                if ph == 0:
                    queries(0, 1, 0, 0, 1)
                finish_last(ph)

            ffn(0)
            attention()
            ffn(1)


_INS = ["L0_attn_x", "L0_attn_Wq", "L0_attn_Wkv", "L0_attn_null_kv", "L0_attn_Wout", "L0_ffn_Wq", "L0_ffn_bq", "L0_ffn_Wk",
        "L0_ffn_bk", "L0_ffn_Wv", "L0_ffn_bv", "L0_ffn_Wg1", "L0_ffn_bg1", "L0_ffn_Wg2", "L0_ffn_bg2", "L0_ffn_Wo", "L0_ffn_bo"]


def kernel(**inputs):
    import numpy as _np
    import concourse.bacc as _bacc
    from concourse import mybir as _mybir
    from concourse.bass_utils import run_bass_kernel_spmd as _run

    nc = _bacc.Bacc("TRN2", target_bir_lowering=False, num_devices=1)
    arrays, args = {}, []
    for name in _INS:
        a = _np.ascontiguousarray(inputs[name])
        arrays[f"in_{name}"] = a
        args.append(nc.dram_tensor(f"in_{name}", a.shape, _mybir.dt.from_np(a.dtype), kind="ExternalInput").ap())
    x_shape = inputs["L0_attn_x"].shape
    args.append(nc.dram_tensor("out_0", x_shape, _mybir.dt.float32, kind="ExternalOutput").ap())
    build(nc, *args)
    r = _run(nc, [arrays], core_ids=[0])
    return r.results[0]["out_0"]
```
